# Optimizing a Trainium2 kernel written in Bass

```python
import numpy as np
import jax
import jax.numpy as jnp

def _softmax(x, axis=-1):
    return jax.nn.softmax(x, axis=axis)

def _gelu(x):
    return jax.nn.gelu(x, approximate=True)

def _silu(x):
    return jax.nn.silu(x)

def _sigmoid(x):
    return jax.nn.sigmoid(x)

def _layernorm(x, axis=-1, eps=1e-05):
    m = jnp.mean(x, axis=axis, keepdims=True)
    v = jnp.var(x, axis=axis, keepdims=True)
    return (x - m) / jnp.sqrt(v + eps)

def _scatter_add(tgt, idx, src, axis=0):
    return tgt.at[idx].add(src)

def _segment_sum(src, seg, n):
    return jax.ops.segment_sum(src, seg, n)
kernel_name = 'mk_prb_d1_jaxref_r8_6dbaef'

def setup_inputs(seed: int=0):
    np.random.seed(seed)
    _w = jnp.asarray

    def _L0_attn_setup():
        import jax, jax.numpy as jnp
        import numpy as np
        B, S, E, H = (4, 128, 128, 16)
        D = E // H
        NEG_INF = -1000000000.0

        def _xavier(key, shape, fan_in, fan_out):
            a = (6.0 / (fan_in + fan_out)) ** 0.5
            return jax.random.uniform(key, shape, jnp.float32, -a, a)
        key = jax.random.key(seed)
        kx, kq, kk, kv, ko = jax.random.split(key, 5)
        x = jax.random.normal(kx, (B, S, E), jnp.float32)
        Wq = _xavier(kq, (H, D, D), D, D)
        Wk = _xavier(kk, (H, D, D), D, D)
        Wv = _xavier(kv, (H, D, D), D, D)
        W_O = _xavier(ko, (E, E), E, E)
        return {'x': x, 'Wq': Wq, 'Wk': Wk, 'Wv': Wv, 'W_O': W_O}
    _L0_attn_in = _L0_attn_setup()

    def _L0_ffn_setup():
        import jax, jax.numpy as jnp
        import numpy as np
        DIM = 128
        DEPTH = 6
        HEADS = 16
        DIM_HEAD = 64
        WINDOW = 32
        INNER = HEADS * DIM_HEAD
        DIM_INNER = int(DIM * 4 * 2 / 3)
        QK_SCALE = 8.0

        def shift_tokens(t):
            a, s = jnp.split(t, 2, -1)
            s = jnp.pad(s, ((0, 0), (1, 0), (0, 0)))[:, :-1]
            return jnp.concatenate([a, s], -1)

        def l2norm(t):
            return t / jnp.maximum(jnp.linalg.norm(t, axis=-1, keepdims=True), 1e-12)

        def rotate_half(x):
            x1, x2 = jnp.split(x, 2, -1)
            return jnp.concatenate([-x2, x1], -1)

        def rotary_tables(n):
            half = jnp.arange(0, DIM_HEAD, 2, dtype=jnp.float32)
            inv_freq = 1.0 / 10000.0 ** (half / DIM_HEAD)
            t = jnp.arange(n, dtype=jnp.float32)
            freqs = t[:, None] * inv_freq[None, :]
            freqs = jnp.concatenate([freqs, freqs], -1)
            base_scale = (half + 0.4 * DIM_HEAD) / (1.4 * DIM_HEAD)
            power = (t - n // 2) / (WINDOW // 2)
            scale = base_scale[None, :] ** power[:, None]
            scale = jnp.concatenate([scale, scale], -1)
            return (freqs, scale)

        def local_attention(q, k, v):
            b, h, n, d = q.shape
            w = WINDOW
            nw = n // w
            bq = q.reshape(b, h, nw, w, d)
            bk = k.reshape(b, h, nw, w, d)
            bv = v.reshape(b, h, nw, w, d)

            def look(t):
                p = jnp.pad(t, ((0, 0), (0, 0), (1, 0), (0, 0), (0, 0)))
                return jnp.concatenate([p[:, :, :nw], p[:, :, 1:]], axis=3)
            bk2, bv2 = (look(bk), look(bv))
            seq = jnp.arange(n).reshape(nw, w)
            seq_p = jnp.pad(seq, ((1, 0), (0, 0)), constant_values=-1)
            jt = jnp.concatenate([seq_p[:nw], seq_p[1:]], axis=1)
            it = seq[:, :, None]
            jb = jt[:, None, :]
            mask = (it < jb) | (it > jb + w) | (jb == -1)
            sim = jnp.einsum('bhwie,bhwje->bhwij', bq, bk2) * QK_SCALE
            sim = jnp.where(mask, -jnp.finfo(sim.dtype).max, sim)
            attn = jax.nn.softmax(sim, -1)
            out = jnp.einsum('bhwij,bhwje->bhwie', attn, bv2)
            return out.reshape(b, h, n, d)

        def attn_layer(x, Wqkv, qs, ksc, Wo):
            b, n, _ = x.shape
            qkv = x @ Wqkv
            q, k, v = jnp.split(qkv, 3, -1)
            sh = lambda t: t.reshape(b, n, HEADS, DIM_HEAD).transpose(0, 2, 1, 3)
            q, k, v = (sh(q), sh(k), sh(v))
            q = l2norm(q) * qs
            k = l2norm(k) * ksc
            freqs, scale = rotary_tables(n)
            cos, sin = (jnp.cos(freqs), jnp.sin(freqs))
            q = q * cos * scale + rotate_half(q) * sin * scale
            inv = 1.0 / scale
            k = k * cos * inv + rotate_half(k) * sin * inv
            out = local_attention(q, k, v)
            out = out.transpose(0, 2, 1, 3).reshape(b, n, INNER)
            return out @ Wo

        def ffn_layer(x, g, bln, W1, b1, W2, b2):
            mu = x.mean(-1, keepdims=True)
            var = ((x - mu) ** 2).mean(-1, keepdims=True)
            xn = (x - mu) / jnp.sqrt(var + 1e-05) * g + bln
            hg = xn @ W1 + b1
            a, gate = jnp.split(hg, 2, -1)
            return a * jax.nn.gelu(gate, approximate=False) @ W2 + b2
        key = jax.random.key(seed)
        ks = jax.random.split(key, 8)
        B, N = (2, 256)
        init = lambda k, shape: jax.random.normal(k, shape, jnp.float32) * 0.02
        return {'x': jax.random.normal(ks[0], (B, N, DIM), jnp.float32), 'Wqkv': init(ks[1], (DEPTH, DIM, 3 * INNER)), 'q_scale': jnp.ones((DEPTH, DIM_HEAD), jnp.float32), 'k_scale': jnp.ones((DEPTH, DIM_HEAD), jnp.float32), 'Wo': init(ks[2], (DEPTH, INNER, DIM)), 'ln_g': jnp.ones((DEPTH, DIM), jnp.float32), 'ln_b': jnp.zeros((DEPTH, DIM), jnp.float32), 'W1': init(ks[3], (DEPTH, DIM, 2 * DIM_INNER)), 'b1': jnp.zeros((DEPTH, 2 * DIM_INNER), jnp.float32), 'W2': init(ks[4], (DEPTH, DIM_INNER, DIM)), 'b2': jnp.zeros((DEPTH, DIM), jnp.float32)}
    _L0_ffn_in = _L0_ffn_setup()
    _d = {'L0_attn_x': _L0_attn_in['x'], 'L0_attn_Wq': _L0_attn_in['Wq'], 'L0_attn_Wk': _L0_attn_in['Wk'], 'L0_attn_Wv': _L0_attn_in['Wv'], 'L0_attn_W_O': _L0_attn_in['W_O'], 'L0_ffn_Wqkv': _L0_ffn_in['Wqkv'], 'L0_ffn_q_scale': _L0_ffn_in['q_scale'], 'L0_ffn_k_scale': _L0_ffn_in['k_scale'], 'L0_ffn_Wo': _L0_ffn_in['Wo'], 'L0_ffn_ln_g': _L0_ffn_in['ln_g'], 'L0_ffn_ln_b': _L0_ffn_in['ln_b'], 'L0_ffn_W1': _L0_ffn_in['W1'], 'L0_ffn_b1': _L0_ffn_in['b1'], 'L0_ffn_W2': _L0_ffn_in['W2'], 'L0_ffn_b2': _L0_ffn_in['b2']}
    _x0 = _d['L0_attn_x']
    _d['L0_attn_x'] = jax.random.normal(jax.random.fold_in(jax.random.key(seed), 1), (2, 1024, 128), dtype=_x0.dtype)
    del _x0
    return _d

def reference(L0_attn_x, L0_attn_Wq, L0_attn_Wk, L0_attn_Wv, L0_attn_W_O, L0_ffn_Wqkv, L0_ffn_q_scale, L0_ffn_k_scale, L0_ffn_Wo, L0_ffn_ln_g, L0_ffn_ln_b, L0_ffn_W1, L0_ffn_b1, L0_ffn_W2, L0_ffn_b2):

    def _L0_attn_ref(x, Wq, Wk, Wv, W_O):
        import jax, jax.numpy as jnp
        import numpy as np
        B, S, E, H = (4, 128, 128, 16)
        D = E // H
        NEG_INF = -1000000000.0

        def _xavier(key, shape, fan_in, fan_out):
            a = (6.0 / (fan_in + fan_out)) ** 0.5
            return jax.random.uniform(key, shape, jnp.float32, -a, a)
        b, s, e = x.shape
        h = Wq.shape[0]
        d = e // h
        xh = x.reshape(b, s, h, d).transpose(0, 2, 1, 3)
        Q = jnp.einsum('bhsd,hde->bhse', xh, Wq)
        K = jnp.einsum('bhsd,hde->bhse', xh, Wk)
        V = jnp.einsum('bhsd,hde->bhse', xh, Wv)
        scale = 1.0 / jnp.sqrt(jnp.asarray(d, x.dtype))
        scores = jnp.einsum('bhsd,bhtd->bhst', Q, K) * scale
        causal = jnp.tril(jnp.ones((s, s), bool))
        scores = jnp.where(causal, scores, NEG_INF)
        attn = jax.nn.softmax(scores, axis=-1)
        out = jnp.einsum('bhst,bhtd->bhsd', attn, V)
        cat = out.transpose(0, 2, 1, 3).reshape(b, s, e)
        scrambled = cat.transpose(0, 2, 1).reshape(b, s, e)
        return scrambled @ W_O

    def _L0_ffn_ref(x, Wqkv, q_scale, k_scale, Wo, ln_g, ln_b, W1, b1, W2, b2):
        import jax, jax.numpy as jnp
        import numpy as np
        DIM = 128
        DEPTH = 6
        HEADS = 16
        DIM_HEAD = 64
        WINDOW = 32
        INNER = HEADS * DIM_HEAD
        DIM_INNER = int(DIM * 4 * 2 / 3)
        QK_SCALE = 8.0

        def shift_tokens(t):
            a, s = jnp.split(t, 2, -1)
            s = jnp.pad(s, ((0, 0), (1, 0), (0, 0)))[:, :-1]
            return jnp.concatenate([a, s], -1)

        def l2norm(t):
            return t / jnp.maximum(jnp.linalg.norm(t, axis=-1, keepdims=True), 1e-12)

        def rotate_half(x):
            x1, x2 = jnp.split(x, 2, -1)
            return jnp.concatenate([-x2, x1], -1)

        def rotary_tables(n):
            half = jnp.arange(0, DIM_HEAD, 2, dtype=jnp.float32)
            inv_freq = 1.0 / 10000.0 ** (half / DIM_HEAD)
            t = jnp.arange(n, dtype=jnp.float32)
            freqs = t[:, None] * inv_freq[None, :]
            freqs = jnp.concatenate([freqs, freqs], -1)
            base_scale = (half + 0.4 * DIM_HEAD) / (1.4 * DIM_HEAD)
            power = (t - n // 2) / (WINDOW // 2)
            scale = base_scale[None, :] ** power[:, None]
            scale = jnp.concatenate([scale, scale], -1)
            return (freqs, scale)

        def local_attention(q, k, v):
            b, h, n, d = q.shape
            w = WINDOW
            nw = n // w
            bq = q.reshape(b, h, nw, w, d)
            bk = k.reshape(b, h, nw, w, d)
            bv = v.reshape(b, h, nw, w, d)

            def look(t):
                p = jnp.pad(t, ((0, 0), (0, 0), (1, 0), (0, 0), (0, 0)))
                return jnp.concatenate([p[:, :, :nw], p[:, :, 1:]], axis=3)
            bk2, bv2 = (look(bk), look(bv))
            seq = jnp.arange(n).reshape(nw, w)
            seq_p = jnp.pad(seq, ((1, 0), (0, 0)), constant_values=-1)
            jt = jnp.concatenate([seq_p[:nw], seq_p[1:]], axis=1)
            it = seq[:, :, None]
            jb = jt[:, None, :]
            mask = (it < jb) | (it > jb + w) | (jb == -1)
            sim = jnp.einsum('bhwie,bhwje->bhwij', bq, bk2) * QK_SCALE
            sim = jnp.where(mask, -jnp.finfo(sim.dtype).max, sim)
            attn = jax.nn.softmax(sim, -1)
            out = jnp.einsum('bhwij,bhwje->bhwie', attn, bv2)
            return out.reshape(b, h, n, d)

        def attn_layer(x, Wqkv, qs, ksc, Wo):
            b, n, _ = x.shape
            qkv = x @ Wqkv
            q, k, v = jnp.split(qkv, 3, -1)
            sh = lambda t: t.reshape(b, n, HEADS, DIM_HEAD).transpose(0, 2, 1, 3)
            q, k, v = (sh(q), sh(k), sh(v))
            q = l2norm(q) * qs
            k = l2norm(k) * ksc
            freqs, scale = rotary_tables(n)
            cos, sin = (jnp.cos(freqs), jnp.sin(freqs))
            q = q * cos * scale + rotate_half(q) * sin * scale
            inv = 1.0 / scale
            k = k * cos * inv + rotate_half(k) * sin * inv
            out = local_attention(q, k, v)
            out = out.transpose(0, 2, 1, 3).reshape(b, n, INNER)
            return out @ Wo

        def ffn_layer(x, g, bln, W1, b1, W2, b2):
            mu = x.mean(-1, keepdims=True)
            var = ((x - mu) ** 2).mean(-1, keepdims=True)
            xn = (x - mu) / jnp.sqrt(var + 1e-05) * g + bln
            hg = xn @ W1 + b1
            a, gate = jnp.split(hg, 2, -1)
            return a * jax.nn.gelu(gate, approximate=False) @ W2 + b2
        for i in range(DEPTH):
            x = attn_layer(shift_tokens(x), Wqkv[i], q_scale[i], k_scale[i], Wo[i]) + x
            x = ffn_layer(shift_tokens(x), ln_g[i], ln_b[i], W1[i], b1[i], W2[i], b2[i]) + x
        return x
    x = L0_attn_x
    xn = _layernorm(x, axis=-1)
    x = x + _L0_attn_ref(xn, L0_attn_Wq, L0_attn_Wk, L0_attn_Wv, L0_attn_W_O) + _L0_ffn_ref(xn, L0_ffn_Wqkv, L0_ffn_q_scale, L0_ffn_k_scale, L0_ffn_Wo, L0_ffn_ln_g, L0_ffn_ln_b, L0_ffn_W1, L0_ffn_b1, L0_ffn_W2, L0_ffn_b2)
    return x

_drawn_inputs = setup_inputs


def setup_inputs(seed=0):
    import zlib

    import numpy as np

    out = dict(_drawn_inputs(seed))
    spreads = {'L0_ffn_q_scale': (1.0, 0.6),
     'L0_ffn_k_scale': (1.0, 0.6),
     'L0_ffn_ln_g': (1.0, 0.6),
     'L0_ffn_ln_b': (0.0, 0.8),
     'L0_ffn_b1': (0.0, 0.8),
     'L0_ffn_b2': (0.0, 0.1)}
    factors = {'L0_ffn_W1': 3.713, 'L0_ffn_W2': 3.644}
    for name, (base, spread) in spreads.items():
        noise = np.random.default_rng([zlib.crc32(name.encode()), seed]).standard_normal(out[name].shape)
        drawn = base * np.exp(spread * noise) if base else spread * noise
        out[name] = jnp.asarray(drawn.astype(out[name].dtype))
    for name, factor in factors.items():
        out[name] = (out[name] * factor).astype(out[name].dtype)
    return out
```

```python
from contextlib import ExitStack

import numpy as np

import concourse.bass as bass
from concourse import mybir

F32 = mybir.dt.float32
BF16 = mybir.dt.bfloat16
I32 = mybir.dt.int32
ALU = mybir.AluOpType
ACT = mybir.ActivationFunctionType
AX_X = mybir.AxisListType.X

P = 128
BANK = 512
PAIR = 2 * BANK
EPS = 1e-5
NORM_FLOOR = 1e-12
MASKED = -1e30
RSQRT_MAGIC = float(0x5F3759DF)

A_HEADS = 16
A_DIM = 8
A_SLOT = 32
A_PER_GROUP = P // A_SLOT
A_GROUPS = A_HEADS // A_PER_GROUP

HEADS = 16
HEAD_DIM = 64
HALF = HEAD_DIM // 2
WINDOW = 32
SIM_SCALE = 8.0
INNER = HEADS * HEAD_DIM
CHUNKS = INNER // P
WPT = P // WINDOW
GROUP = 4


def rotary_constants(n):
    f = np.float32
    half = np.arange(0, HEAD_DIM, 2, dtype=f)
    inv_freq = f(1.0) / np.power(f(10000.0), half / f(HEAD_DIM)).astype(f)
    t = np.arange(n, dtype=f)
    freqs = (t[:, None] * inv_freq[None, :]).astype(f)
    base = (half + f(0.4 * HEAD_DIM)) / f(1.4 * HEAD_DIM)
    power = (t - f(n // 2)) / f(WINDOW // 2)
    scale = np.power(base[None, :], power[:, None]).astype(f)
    cos, sin = np.cos(freqs), np.sin(freqs)
    tab_c = np.zeros((n, 2, HEAD_DIM), f)
    tab_s = np.zeros((n, 2, HEAD_DIM), f)
    for m, s in enumerate((scale, f(1.0) / scale)):
        tab_c[:, m, :HALF] = tab_c[:, m, HALF:] = cos * s
        tab_s[:, m, :HALF] = -sin * s
        tab_s[:, m, HALF:] = sin * s
    return tab_c, tab_s


def mask_constants():
    i = np.arange(P)
    ident = np.eye(P, dtype=np.float32)
    rows = np.where(i[None, :] <= i[:, None], 0.0, MASKED).astype(np.float32)
    r = (i % WINDOW)[:, None]
    k = np.arange(2 * WINDOW)[None, :]
    win = np.where((k >= r) & (k <= r + WINDOW), 0.0, MASKED).astype(np.float32)
    win0 = win.copy()
    win0[:WINDOW, :WINDOW] = MASKED
    one_row = ((i % A_SLOT) == A_DIM).astype(np.float32)[:, None]
    return np.concatenate([ident, rows, rows.T, win, win0, one_row], axis=1)


class Program:

    def __init__(self, nc, ctx):
        self.nc, self.ctx = nc, ctx
        self.queues = {e: [] for e in ("tensor", "vector", "scalar", "gpsimd", "sync")}
        self.done = {e: ctx.enter_context(nc.semaphore(f"{e}_done")) for e in ("tensor", "vector", "scalar", "gpsimd")}
        self.count = {e: 0 for e in self.done}
        self.seen = {e: {} for e in self.queues}
        self.dma = {}

    def wait(self, engine, marks):
        for key, sem, value in marks:
            if self.seen[engine].get(key, 0) < value:
                self.seen[engine][key] = value
                self.queues[engine].append(lambda e, sem=sem, value=value: e.wait_ge(sem, value))

    def run(self, engine, instruction, after=(), mark=True):
        self.wait(engine, after)
        if engine != "tensor" and self.count[engine]:
            self.wait(engine, [(engine, self.done[engine], self.count[engine])])
        if not mark:
            self.queues[engine].append(instruction)
            return None
        self.count[engine] += 1
        sem = self.done[engine]
        self.queues[engine].append(lambda e: instruction(e).then_inc(sem, 1))
        return (engine, sem, self.count[engine])

    def load(self, stream, out, in_, after=(), engine="sync"):
        if stream not in self.dma:
            self.dma[stream] = [self.ctx.enter_context(self.nc.semaphore(f"dma_{stream}")), 0]
        entry = self.dma[stream]
        entry[1] += 16
        sem = entry[0]
        self.wait(engine, after)
        self.queues[engine].append(lambda e: e.dma_start(out, in_).then_inc(sem, 16))
        return (f"dma_{stream}", sem, entry[1])

    def emit(self, block):
        for name in self.queues:
            def body(engine, queue=self.queues[name]):
                for instruction in queue:
                    instruction(engine)
            {"tensor": block.tensor, "vector": block.vector, "scalar": block.scalar,
             "gpsimd": block.gpsimd, "sync": block.sync}[name](body)


def build(nc, ins, out, scratch):
    x, consts, tab_c, tab_s = ins["x"], ins["consts"], ins["tab_c"], ins["tab_s"]
    batches, seq, dim = x.shape
    layers = ins["Wqkv"].shape[0]
    tiles = seq // P
    all_tiles = batches * tiles
    ff = ins["W2"].shape[1]
    ff_rows = [min(P, ff - P * c) for c in range((ff + P - 1) // P)]
    assert dim == P and ins["Wqkv"].shape[2] == 3 * INNER

    with ExitStack() as ctx:
        prog = Program(nc, ctx)
        run, load = prog.run, prog.load

        def sb(name, shape, dt=F32):
            return ctx.enter_context(nc.sbuf_tensor(name, shape, dt))

        banks = ctx.enter_context(nc.psum_tensor("banks", [P, 4, PAIR], F32))
        free_pairs = [(i, []) for i in range(4)]

        def take():
            i, marks = free_pairs.pop(0)
            return i, banks[:, i, :], marks

        def give(i, *marks):
            free_pairs.append((i, list(marks)))

        cst = sb("cst", [P, consts.shape[1]])
        ident = cst[:, 0:P]
        one_row = cst[:, 3 * P + 4 * WINDOW:3 * P + 4 * WINDOW + 1]
        cst_b = sb("cst_b", [P, 3 * P + 4 * WINDOW], BF16)
        ident_b = cst_b[:, 0:P]
        mask_rows, mask_cols = cst_b[:, P:2 * P], cst_b[:, 2 * P:3 * P]
        win_b = sb("win_b", [P, 2, 8, 2 * WINDOW], BF16)
        base_c, base_s = sb("base_c", [P, tiles, 2, HEAD_DIM]), sb("base_s", [P, tiles, 2, HEAD_DIM])
        c_loaded = load("const", cst[:, :], consts)
        X = sb("X", [P, all_tiles, P])
        x_loaded = load("x", X[:, :, :], x.rearrange("b (t p) d -> p (b t) d", p=P))
        for tab, src in ((base_c, tab_c), (base_s, tab_s)):
            tabs_loaded = load("tabs", tab[:, :, :, :], src.rearrange("(t p) m d -> p t m d", p=P))
        c_ready = run("vector", lambda e: e.tensor_copy(cst_b[:, :], cst[:, 0:3 * P + 4 * WINDOW]), [c_loaded])
        for m in range(2):
            at = 3 * P + 2 * WINDOW * m
            c_ready = run("vector", lambda e, m=m, at=at: e.tensor_copy(
                win_b[:, m, :, :], cst_b[:, at:at + 2 * WINDOW].unsqueeze(1).to_broadcast([P, 8, 2 * WINDOW])))

        RS = P
        rs_h, rs_t = sb("rs_h", [P, RS], I32), sb("rs_t", [P, RS])

        def rsqrt(y, v, n, after=()):
            h, t = rs_h[:, 0:n], rs_t[:, 0:n]
            run("vector", lambda e: e.tensor_scalar(h, v.bitcast(I32), 1, None, ALU.logical_shift_right), after)
            run("vector", lambda e: e.tensor_scalar(y.bitcast(I32), h, -1.0, RSQRT_MAGIC, ALU.mult, ALU.add))
            for _ in range(3):
                run("vector", lambda e: e.tensor_tensor(t, y, y, ALU.mult))
                run("vector", lambda e: e.scalar_tensor_tensor(out=t, in0=t, scalar=-0.5, in1=v, op0=ALU.mult, op1=ALU.mult))
                last = run("vector", lambda e: e.scalar_tensor_tensor(out=y, in0=t, scalar=1.5, in1=y, op0=ALU.add, op1=ALU.mult))
            return last

        stats = sb("stats", [P, 6])
        mean_var = sb("mean_var", [P, all_tiles, 2])
        ln_v, ln_r = sb("ln_v", [P, all_tiles]), sb("ln_r", [P, all_tiles])

        def norm_tiles(src, dst, n, after):
            for i in range(n):
                run("vector", lambda e, i=i: e.bn_stats(stats[:, :], src[:, i, :]), after if i == 0 else ())
                run("vector", lambda e, i=i: e.bn_aggr(mean_var[:, i, :], stats[:, :]))
            run("vector", lambda e: e.tensor_scalar(ln_v[:, 0:n], mean_var[:, 0:n, 1], EPS, None, ALU.add))
            rsqrt(ln_r[:, 0:n], ln_v[:, 0:n], n)
            for i in range(n):
                last = run("vector", lambda e, i=i: e.tensor_scalar(
                    dst[:, i, :], src[:, i, :], mean_var[:, i, 0:1], ln_r[:, i:i + 1], ALU.subtract, ALU.mult))
            return last

        x_ready = [norm_tiles(X, X, all_tiles, [x_loaded])] * all_tiles

        qk_raw = sb("qk_raw", [P, 2, INNER])
        qk_tmp = sb("qk_tmp", [P, 2, INNER])
        qk_rot = sb("qk_rot", [P, 2, INNER])
        PTc = sb("PTc", [P, HEADS, P])
        PTp = sb("PTp", [P, HEADS, P])
        cat = sb("cat", [P, all_tiles, P])
        VV = sb("VV", [P, 5, INNER])
        ON, OT = sb("ON", [P, INNER]), sb("OT", [P, CHUNKS, P])

        w_pad = [sb(f"w_pad{m}", [P, A_HEADS, A_SLOT]) for m in range(3)]
        w_out_a = sb("w_out_a", [P, P])
        VA = VV[:, 0:4, :].rearrange("p a (t h d) -> p (a t) h d", h=A_HEADS, d=A_SLOT)
        QA, KA = ON, OT[:, :, :].rearrange("p c q -> p (c q)")
        m_neg = sb("m_neg", [P, tiles, P])
        a_sum = sb("a_sum", [P, tiles, A_PER_GROUP])
        xnT = qk_raw[:, 0, :]
        pt_ring = [qk_tmp[:, 0, :], qk_tmp[:, 1, :], qk_rot[:, 0, :], qk_rot[:, 1, :]]
        accT = qk_raw[:, 1, :]
        xa = PTc[:, 0:tiles, :]
        ya = PTp[:, 0:tiles, :]

        zeroed = None
        for m in range(3):
            zeroed = run("gpsimd", lambda e, m=m: e.memset(w_pad[m][:, :, :], 0.0))
        m_neg_ready = run("gpsimd", lambda e: e.memset(m_neg[:, :, :], 0.0))
        for m, name in enumerate(("Wq", "Wk", "Wv")):
            for h in range(A_HEADS):
                w_loaded = load(f"w_pad{m}", w_pad[m][A_DIM * h:A_DIM * (h + 1), h, 0:A_DIM], ins[name][h], [zeroed],
                                engine=("sync", "scalar")[h % 2])
        w_marks = [("dma_w_pad%d" % m, prog.dma[f"w_pad{m}"][0], prog.dma[f"w_pad{m}"][1]) for m in range(3)]
        wo_a_loaded = load("w_out_a", w_out_a[:, :], ins["W_O"])
        pt_free = [[], [], [], []]
        pt_turn = 0
        xnT_free, acc_free, VA_free, QA_free, KA_free = [], [], [], [], []
        cat_ready = {}

        for b in range(batches):
            i, ps, marks = take()
            for t in range(tiles):
                tok = run("tensor", lambda e, ps=ps, t=t, b=b: e.transpose(ps[:, P * t:P * (t + 1)], X[:, b * tiles + t, :], ident),
                          marks + [c_loaded, x_ready[b * tiles + t]] if t == 0 else ())
            xnT_ready = run("scalar", lambda e, ps=ps: e.copy(xnT, ps), [tok] + xnT_free)
            give(i, xnT_ready)
            xnT_free = []
            for t in range(tiles):
                i, ps, marks = take()
                tok = run("tensor", lambda e, ps=ps, t=t: e.matmul(
                    ps[:, 0:BANK], xnT[:, P * t:P * (t + 1)], w_pad[2][:, :, :].rearrange("p h d -> p (h d)"),
                    start=True, stop=True), marks + [xnT_ready, w_marks[2]])
                va = run("scalar", lambda e, ps=ps, t=t: e.copy(VA[:, t, :, :].rearrange("p h d -> p (h d)"), ps[:, 0:BANK]),
                         [tok] + VA_free)
                give(i, va)
            VA_ready = run("gpsimd", lambda e: e.memset(VA[:, :, :, A_DIM:A_DIM + 1], 1.0), [va])
            VA_free = []
            for g in range(A_GROUPS):
                lo = g * P
                for m, dst in ((0, QA), (1, KA)):
                    i, ps, marks = take()
                    for c in range(seq // BANK):
                        tok = run("tensor", lambda e, ps=ps, m=m, c=c, lo=lo: e.matmul(
                            ps[:, BANK * c:BANK * (c + 1)], w_pad[m][:, :, :].rearrange("p h d -> p (h d)")[:, lo:lo + P],
                            xnT[:, BANK * c:BANK * (c + 1)], start=True, stop=True), marks + [xnT_ready, w_marks[m]])
                    if m == 0:
                        q_ready = run("scalar", lambda e, ps=ps: e.copy(QA[:, :], ps), [tok] + QA_free)
                        give(i, q_ready)
                    else:
                        k_ready = run("scalar", lambda e, ps=ps: e.activation(KA[:, :], ps, ACT.Identity, bias=one_row),
                                      [tok, c_loaded] + KA_free)
                        give(i, k_ready)
                for qt in range(tiles):
                    for j in range(A_PER_GROUP):
                        r = slice(A_SLOT * j, A_SLOT * j + A_DIM)
                        i, ps, marks = take()
                        n = P * (qt + 1)
                        for c in range((n + BANK - 1) // BANK):
                            e1 = min(n, BANK * (c + 1))
                            tok = run("tensor", lambda e, ps=ps, r=r, qt=qt, c=c, e1=e1: e.matmul(
                                ps[:, BANK * c:e1], QA[r, P * qt:P * (qt + 1)], KA[r, BANK * c:e1], start=True, stop=True),
                                marks + [q_ready, k_ready])
                        tok = run("tensor", lambda e, ps=ps, n=n: e.matmul(ps[:, n - P:n], ident_b, mask_rows, start=False, stop=True,
                                                                                     skip_group_check=True),
                                  [c_ready])
                        mx = run("vector", lambda e, ps=ps, n=n, qt=qt, j=j: e.tensor_reduce(
                            m_neg[:, qt, A_SLOT * j + A_DIM:A_SLOT * j + A_DIM + 1], ps[:, 0:n], AX_X, ALU.max, negate=True),
                            [tok, m_neg_ready])
                        give(i, mx)
                i, ps, marks = take()
                for t in range(tiles):
                    tok = run("tensor", lambda e, ps=ps, t=t: e.transpose(ps[:, P * t:P * (t + 1)], m_neg[:, t, :], ident),
                              marks + [mx])
                m_neg_ready = tok
                q_ready = run("vector", lambda e, ps=ps: e.tensor_tensor(QA[:, :], ps, QA[:, :], ALU.add), [tok])
                give(i, q_ready)
                acc_i, acc, acc_marks = take()
                for kt in range(tiles):
                    q0 = P * kt
                    for j in range(A_PER_GROUP):
                        r = slice(A_SLOT * j, A_SLOT * j + A_DIM + 1)
                        h = g * A_PER_GROUP + j
                        i, ps, marks = take()
                        spans = [(max(q0, BANK * c), BANK * (c + 1)) for c in range(seq // BANK) if q0 < BANK * (c + 1)]
                        for s0, s1 in spans:
                            tok = run("tensor", lambda e, ps=ps, r=r, kt=kt, s0=s0, s1=s1, q0=q0: e.matmul(
                                ps[:, s0:s1], KA[r, P * kt:P * (kt + 1)], QA[r, s0:s1], start=True, stop=True),
                                marks + [q_ready, k_ready])
                            if s0 == q0:
                                tok = run("tensor", lambda e, ps=ps, q0=q0: e.matmul(
                                    ps[:, q0:q0 + P], ident_b, mask_cols, start=False, stop=True, skip_group_check=True))
                        buf, was = pt_ring[pt_turn], pt_free[pt_turn]
                        ex = run("scalar", lambda e, ps=ps, buf=buf, q0=q0: e.activation(
                            buf[:, q0:seq], ps[:, q0:seq], ACT.Exp, scale=float(A_DIM) ** -0.5), [tok] + was)
                        give(i, ex)
                        for s0, s1 in spans:
                            tok = run("tensor", lambda e, acc=acc, j=j, kt=kt, h=h, buf=buf, s0=s0, s1=s1: e.matmul(
                                acc[A_SLOT * j:A_SLOT * (j + 1), s0:s1], VA[:, kt, h, :], buf[:, s0:s1],
                                start=kt == 0, stop=True, skip_group_check=True), acc_marks + [ex, VA_ready])
                        pt_free[pt_turn] = [tok]
                        pt_turn = (pt_turn + 1) % 4
                QA_free, KA_free = [tok], [tok]
                at = run("scalar", lambda e, acc=acc: e.copy(accT, acc), [tok] + acc_free)
                give(acc_i, at)
                i, ps, marks = take()
                for t in range(tiles):
                    tok = run("tensor", lambda e, ps=ps, t=t: e.transpose(ps[:, P * t:P * (t + 1)], accT[:, P * t:P * (t + 1)], ident),
                              marks + [at])
                acc_free = [tok]
                psv = ps.rearrange("p (t j c) -> p t j c", j=A_PER_GROUP, c=A_SLOT)
                run("vector", lambda e, psv=psv: e.reciprocal(a_sum[:, :, :], psv[:, :, :, A_DIM]), [tok])
                last = run("vector", lambda e, psv=psv, b=b, g=g: e.tensor_tensor(
                    cat[:, b * tiles:(b + 1) * tiles, :].rearrange("p t (g j d) -> p t g j d", j=A_PER_GROUP, d=A_DIM)[:, :, g],
                    psv[:, :, :, 0:A_DIM], a_sum[:, :, :].unsqueeze(3).to_broadcast([P, tiles, A_PER_GROUP, A_DIM]), ALU.mult))
                give(i, last)
            VA_free = [tok]
            xnT_free = [tok]
            xa_free = [] if b == 0 else [ya_stored]
            xa_loaded = load("xa", xa, x[b].rearrange("(e t) d -> e t d", t=tiles), xa_free + ([] if b == 0 else [y_ready]))
            i, ps, marks = take()
            for t in range(tiles):
                tok = run("tensor", lambda e, ps=ps, t=t, b=b: e.matmul(
                    ps[:, P * t:P * (t + 1)], cat[:, b * tiles + t, :], w_out_a[:, :], start=True, stop=True),
                    marks + [last, wo_a_loaded])
            y_ready = run("vector", lambda e, ps=ps: e.tensor_tensor(
                ya.rearrange("p t d -> p (t d)"), ps, xa.rearrange("p t d -> p (t d)"), ALU.add), [tok, xa_loaded] + xa_free)
            give(i, y_ready)
            ya_stored = load("ya", scratch[b].rearrange("(e t) d -> e t d", t=tiles), ya, [y_ready])
        YA = cat
        ya_loaded = load("ya_back", YA[:, :, :], scratch.rearrange("b (t p) d -> p (b t) d", p=P), [ya_stored, tok])

        w_qkv = [sb(f"w_qkv{s}", [P, 3 * INNER]) for s in range(1)]
        w_o = [sb(f"w_o{s}", [P, CHUNKS, P]) for s in range(2)]
        w_1 = [sb(f"w_1{s}", [P, 2 * ff]) for s in range(2)]
        w_2 = [sb(f"w_2{s}", [P, len(ff_rows), P]) for s in range(2)]
        vecs = [sb(f"vecs{s}", [P, 2 + 2 * len(ff_rows)]) for s in range(2)]
        b2_all = [sb(f"b2_all{s}", [P, P]) for s in range(2)]
        qk_gain = sb("qk_gain", [P, 2, HEAD_DIM])
        tab_cl, tab_sl = sb("tab_cl", [P, tiles, 2, HEAD_DIM]), sb("tab_sl", [P, tiles, 2, HEAD_DIM])
        xsT = [sb(f"xsT{b}", [P, seq + 1]) for b in range(batches)]
        xfT = [sb(f"xfT{b}", [P, seq + 1]) for b in range(batches)]
        QT = sb("QT", [P, CHUNKS, P])
        KT = [sb(f"KT{s}", [P, CHUNKS, WINDOW + P]) for s in range(2)]
        V, Vp = [VV[:, s, :] for s in range(3)], [VV[:, 3 + s, :] for s in range(2)]
        PB = sb("PB", [P, HEADS, 2 * WINDOW])
        ss, rn = sb("ss", [P, 2 * HEADS]), sb("rn", [P, 2 * HEADS])
        mx_t, sm_t, rs_o = sb("mx_t", [P, HEADS]), sb("sm_t", [P, HEADS]), sb("rs_o", [P, HEADS])
        xf_n, xf_T = sb("xf_n", [P, GROUP, P]), sb("xf_T", [P, GROUP * P])
        gel, uT = sb("gel", [P, GROUP * P]), sb("uT", [P, len(ff_rows), GROUP * P])

        m0 = run("gpsimd", lambda e: e.memset(PTc[:, :, :], 0.0), [y_ready, ya_stored])
        m0 = run("gpsimd", lambda e: e.memset(PTp[:, :, :], 0.0), [ya_stored])
        for b in range(batches):
            for buf in (xsT[b], xfT[b]):
                m0 = run("gpsimd", lambda e, buf=buf: e.memset(buf[HEAD_DIM:P, 0:1], 0.0))
        zero_ready = m0

        W = {}
        layer_end = {}
        used = {"qkv": [], "tabs": []}

        def load_layer(l):
            s = l % 2
            free = layer_end.get(l - 2, [])
            load(f"w{s}", w_o[s][:, :, :], ins["Wo"][l].rearrange("(c p) d -> p c d", p=P), free)
            load(f"w{s}", w_1[s][:, :], ins["W1"][l])
            for c, n in enumerate(ff_rows):
                load(f"w{s}", w_2[s][0:n, c, :], ins["W2"][l, P * c:P * c + n, :])
                for m in range(2):
                    at = m * ff + P * c
                    load(f"w{s}", vecs[s][0:n, 2 + m * len(ff_rows) + c:3 + m * len(ff_rows) + c],
                         ins["b1"][l, at:at + n].rearrange("(p a) -> p a", a=1))
            load(f"w{s}", vecs[s][:, 0:1], ins["ln_g"][l].rearrange("(p a) -> p a", a=1))
            load(f"w{s}", vecs[s][:, 1:2], ins["ln_b"][l].rearrange("(p a) -> p a", a=1))
            W[l] = load(f"w{s}", b2_all[s][:, :], ins["b2"][l:l + 1, :].to_broadcast([P, P]))

        def load_qkv(l):
            done = load("qkv", w_qkv[0][:, :], ins["Wqkv"][l], used["qkv"])
            load("gain", qk_gain[:, 0, :], ins["q_scale"][l:l + 1, :].to_broadcast([P, HEAD_DIM]), used["tabs"])
            gain = load("gain", qk_gain[:, 1, :], ins["k_scale"][l:l + 1, :].to_broadcast([P, HEAD_DIM]))
            g = qk_gain[:, :, :].unsqueeze(1).to_broadcast([P, tiles, 2, HEAD_DIM])
            run("gpsimd", lambda e: e.tensor_tensor(tab_cl[:, :, :, :], base_c[:, :, :, :], g, ALU.mult), [gain, tabs_loaded] + used["tabs"])
            for d, s in ((0, HALF), (HALF, 0)):
                gs = qk_gain[:, :, s:s + HALF].unsqueeze(1).to_broadcast([P, tiles, 2, HALF])
                tabs = run("gpsimd", lambda e, d=d, gs=gs: e.tensor_tensor(
                    tab_sl[:, :, :, d:d + HALF], base_s[:, :, :, d:d + HALF], gs, ALU.mult))
            used["tabs"] = [tabs]
            return done, tabs

        def shifted(dst, b, half, after, free):
            i, ps, marks = take()
            for k in range(GROUP):
                t = b * tiles + half * GROUP + k
                tok = run("tensor", lambda e, ps=ps, k=k, t=t: e.transpose(ps[:, P * k:P * (k + 1)], X[:, t, :], ident),
                          marks + [x_ready[t]] + after)
            c0 = half * GROUP * P
            run("scalar", lambda e: e.copy(dst[0:64, c0:c0 + GROUP * P], ps[0:64, 0:GROUP * P]), [tok, zero_ready] + free)
            done = run("scalar", lambda e: e.copy(dst[64:P, c0 + 1:c0 + 1 + GROUP * P], ps[64:P, 0:GROUP * P]))
            give(i, done)
            return done

        was_a = [y_ready, tok]
        st = {"V": [was_a] * 3, "Vp": [was_a] * 2, "KT": [[], []], "KTready": [None, None],
              "raw": was_a, "tmp": was_a, "rot0": was_a, "rot1": was_a, "PT": [], "PB": [], "QT": [], "ON": was_a, "OT": was_a,
              "n": 0}

        def attention_tile(l, b, t, qkv_ready, tabs_ready, xs_ready):
            n = st["n"]
            st["n"] += 1
            s = l % 2
            first = t == 0
            lhs = xsT[b][:, P * t:P * (t + 1)]
            squares = []
            for m in range(2):
                i, ps, marks = take()
                for c in range(2):
                    at = m * INNER + BANK * c
                    tok = run("tensor", lambda e, ps=ps, c=c, at=at: e.matmul(
                        ps[:, BANK * c:BANK * (c + 1)], lhs, w_qkv[0][:, at:at + BANK], start=True, stop=True),
                        marks + [qkv_ready, xs_ready])
                run("scalar", lambda e, ps=ps, m=m: e.copy(qk_raw[:, m, :], ps), [tok] + st["raw"])
                sq = run("scalar", lambda e, ps=ps, m=m: e.activation(qk_tmp[:, m, :], ps, ACT.Square), st["tmp"])
                give(i, sq)
            yield
            i, ps, marks = take()
            for c in range(2):
                at = 2 * INNER + BANK * c
                tok = run("tensor", lambda e, ps=ps, c=c, at=at: e.matmul(
                    ps[:, BANK * c:BANK * (c + 1)], lhs, w_qkv[0][:, at:at + BANK], start=True, stop=True), marks)
            used["qkv"] = [tok]
            v, vp = V[n % 3], Vp[n % 2]
            v_ready = run("scalar", lambda e, ps=ps: e.copy(v, ps), [tok] + st["V"][n % 3])
            give(i, v_ready)
            if first:
                vp_ready = run("gpsimd", lambda e: e.memset(vp[0:WINDOW, :], 0.0), st["Vp"][n % 2])
                vp_marks = [vp_ready]
            else:
                prev = V[(n - 1) % 3]
                vp_marks = [load(f"vp{n % 2}", vp[0:WINDOW, :], prev[P - WINDOW:P, :], st["Vp"][n % 2])]
            vp_marks.append(load(f"vp{n % 2}", vp[WINDOW:P, :], v[0:P - WINDOW, :], [v_ready] + st["Vp"][n % 2]))
            run("vector", lambda e: e.tensor_reduce(ss[:, :], qk_tmp[:, :, :].rearrange("p m (h d) -> p (m h) d", d=HEAD_DIM),
                                                    AX_X, ALU.add), [sq])
            run("vector", lambda e: e.tensor_scalar(ss[:, :], ss[:, :], NORM_FLOOR ** 2, None, ALU.max))
            rsqrt(rn[:, :], ss[:, :], 2 * HEADS)
            qn = run("vector", lambda e: e.tensor_tensor(
                qk_raw[:, :, :].rearrange("p m (h d) -> p (m h) d", d=HEAD_DIM),
                qk_raw[:, :, :].rearrange("p m (h d) -> p (m h) d", d=HEAD_DIM),
                rn[:, :].unsqueeze(2).to_broadcast([P, 2 * HEADS, HEAD_DIM]), ALU.mult))
            yield
            for m in range(2):
                for d, o in ((0, HALF), (HALF, 0)):
                    src = qk_raw[:, m, :].rearrange("p (h d) -> p h d", d=HEAD_DIM)[:, :, o:o + HALF]
                    dst = qk_tmp[:, m, :].rearrange("p (h d) -> p h d", d=HEAD_DIM)[:, :, d:d + HALF]
                    tb = tab_sl[:, t, m, d:d + HALF].unsqueeze(1).to_broadcast([P, HEADS, HALF])
                    sw = run("gpsimd", lambda e, dst=dst, src=src, tb=tb: e.tensor_tensor(dst, src, tb, ALU.mult), [qn, tabs_ready])
                run("vector", lambda e, m=m: e.tensor_tensor(
                    qk_rot[:, m, :].rearrange("p (h d) -> p h d", d=HEAD_DIM),
                    qk_raw[:, m, :].rearrange("p (h d) -> p h d", d=HEAD_DIM),
                    tab_cl[:, t, m, :].unsqueeze(1).to_broadcast([P, HEADS, HEAD_DIM]), ALU.mult),
                    [tabs_ready] + st["rot%d" % m])
            used["tabs"] = [sw, qn]
            rot = []
            for m in range(2):
                rot.append(run("vector", lambda e, m=m: e.tensor_tensor(qk_rot[:, m, :], qk_rot[:, m, :], qk_tmp[:, m, :], ALU.add), [sw]))
            used["tabs"] = [sw, rot[1]]
            st["raw"], st["tmp"] = [sw, rot[1]], [rot[1]]
            yield
            kt_buf = KT[n % 2]
            for m in (1, 0):
                i, ps, marks = take()
                for c in range(CHUNKS):
                    tok = run("tensor", lambda e, ps=ps, c=c, m=m: e.transpose(
                        ps[:, P * c:P * (c + 1)], qk_rot[:, m, P * c:P * (c + 1)], ident), marks + [rot[m]])
                st["rot%d" % m] = [tok]
                if m:
                    k_ready = run("scalar", lambda e, ps=ps: e.copy(
                        kt_buf[:, :, WINDOW:WINDOW + P], ps.rearrange("p (c q) -> p c q", q=P)), [tok] + st["KT"][n % 2])
                    give(i, k_ready)
                else:
                    q_ready = run("scalar", lambda e, ps=ps: e.copy(QT[:, :, :].rearrange("p c q -> p (c q)"), ps), [tok] + st["QT"])
                    give(i, q_ready)
            if first:
                kp = run("gpsimd", lambda e: e.memset(kt_buf[:, :, 0:WINDOW], 0.0), st["KT"][n % 2])
            else:
                before = KT[(n - 1) % 2]
                kp = run("gpsimd", lambda e: e.tensor_copy(kt_buf[:, :, 0:WINDOW], before[:, :, P:P + WINDOW]),
                         st["KT"][n % 2] + [st["KTready"][(n - 1) % 2]])
            st["KTready"][n % 2] = k_ready
            yield
            i, ps, marks = take()
            for half in range(2):
                run("tensor", lambda e, ps=ps, half=half: e.matmul(
                    ps[:, BANK * half:BANK * (half + 1)], ident_b, win_b[:, int(first), :, :].rearrange("p c k -> p (c k)"),
                    start=True, stop=True), marks + [c_ready], mark=False)
            for c in range(CHUNKS):
                for w in range(WPT):
                    for half in range(2):
                        r = slice(64 * half, 64 * half + 64)
                        col = BANK * half + 2 * WINDOW * c
                        fin = c == CHUNKS - 1
                        tok = run("tensor", lambda e, ps=ps, r=r, c=c, w=w, col=col, fin=fin: e.matmul(
                            ps[WINDOW * w:WINDOW * (w + 1), col:col + 2 * WINDOW], QT[r, c, WINDOW * w:WINDOW * (w + 1)],
                            kt_buf[r, c, WINDOW * w:WINDOW * (w + 2)], start=False, stop=True, skip_group_check=True),
                            [q_ready, k_ready, kp], mark=fin and w == WPT - 1 and half == 1)
            st["QT"] = [tok]
            st["KT"][n % 2] = [tok]
            st["KT"][(n - 1) % 2] = st["KT"][(n - 1) % 2] + [kp]
            yield
            sc = ps.rearrange("p (h k) -> p h k", k=2 * WINDOW)
            run("vector", lambda e: e.tensor_reduce(mx_t[:, :], sc, AX_X, ALU.max), [tok])
            sub = run("vector", lambda e: e.tensor_tensor(PB[:, :, :], sc, mx_t[:, :].unsqueeze(2).to_broadcast([P, HEADS, 2 * WINDOW]),
                                                          ALU.subtract), st["PB"])
            give(i, sub)
            ex = run("scalar", lambda e: e.activation(PB[:, :, :], PB[:, :, :], ACT.Exp, scale=SIM_SCALE), [sub])
            yield
            for w in range(WPT):
                r = slice(WINDOW * w, WINDOW * (w + 1))
                for src, dst in ((0, PTp), (WINDOW, PTc)):
                    pt = run("vector", lambda e, r=r, src=src, dst=dst: e.transpose(
                        dst[r, :, r], PB[r, :, src:src + WINDOW]), [ex, zero_ready] + st["PT"])
            run("vector", lambda e: e.tensor_reduce(sm_t[:, :], PB[:, :, :], AX_X, ALU.add))
            rcp = run("vector", lambda e: e.reciprocal(rs_o[:, :], sm_t[:, :]))
            st["PB"] = [rcp]
            yield
            i, ps, marks = take()
            for half in range(2):
                for c in range(CHUNKS):
                    hh = half * CHUNKS + c
                    o = ps[:, BANK * half + HEAD_DIM * c:BANK * half + HEAD_DIM * (c + 1)]
                    vs = slice(HEAD_DIM * (2 * c + half), HEAD_DIM * (2 * c + half + 1))
                    run("tensor", lambda e, o=o, hh=hh, vs=vs: e.matmul(o, PTc[:, hh, :], v[:, vs], start=True, stop=False),
                        marks + [pt, v_ready], mark=False)
                    tok = run("tensor", lambda e, o=o, hh=hh, vs=vs: e.matmul(o, PTp[:, hh, :], vp[:, vs], start=False, stop=True),
                              vp_marks, mark=hh == HEADS - 1)
            st["PT"] = [tok]
            st["V"][n % 3] = [tok, vp_marks[-1]]
            if not first:
                st["V"][(n - 1) % 3] = st["V"][(n - 1) % 3] + [vp_marks[0]]
            st["Vp"][n % 2] = [tok]
            on = run("vector", lambda e, ps=ps: e.tensor_tensor(
                ON[:, :].rearrange("p (c f d) -> p f c d", f=2, d=HEAD_DIM),
                ps.rearrange("p (f c d) -> p f c d", f=2, d=HEAD_DIM),
                rs_o[:, :].rearrange("p (f c) -> p f c", f=2).unsqueeze(3).to_broadcast([P, 2, CHUNKS, HEAD_DIM]), ALU.mult),
                [tok] + st["ON"])
            give(i, on)
            yield
            i, ps, marks = take()
            for c in range(CHUNKS):
                tok = run("tensor", lambda e, ps=ps, c=c: e.transpose(ps[:, P * c:P * (c + 1)], ON[:, P * c:P * (c + 1)], ident),
                          marks + [on])
            st["ON"] = [tok]
            ot = run("scalar", lambda e, ps=ps: e.copy(OT[:, :, :].rearrange("p c q -> p (c q)"), ps), [tok] + st["OT"])
            give(i, ot)
            yield
            i, ps, marks = take()
            for c in range(CHUNKS):
                tok = run("tensor", lambda e, ps=ps, c=c: e.matmul(ps[:, 0:P], OT[:, c, :], w_o[s][:, c, :], start=c == 0,
                                                                   stop=c == CHUNKS - 1), marks + [ot, W[l]])
            st["OT"] = [tok]
            x_ready[b * tiles + t] = run("vector", lambda e, ps=ps: e.tensor_tensor(
                X[:, b * tiles + t, :], ps[:, 0:P], X[:, b * tiles + t, :], ALU.add), [tok])
            give(i, x_ready[b * tiles + t])

        fst = {"xfT": [[], []], "xf_n": [], "xf_T": [], "gel": [], "uT": []}

        def feed_forward(l, b, half):
            s = l % 2
            xf = shifted(xfT[b], b, half, [], fst["xfT"][b])
            c0 = half * GROUP * P
            i, ps, marks = take()
            for k in range(GROUP):
                tok = run("tensor", lambda e, ps=ps, k=k: e.transpose(
                    ps[:, P * k:P * (k + 1)], xfT[b][:, c0 + P * k:c0 + P * (k + 1)], ident), marks + [xf])
            fst["xfT"][b] = [tok]
            nd = norm_tiles(ps.rearrange("p (t d) -> p t d", d=P), xf_n, GROUP, [tok] + fst["xf_n"])
            give(i, nd)
            yield
            i, ps, marks = take()
            for k in range(GROUP):
                tok = run("tensor", lambda e, ps=ps, k=k: e.transpose(ps[:, P * k:P * (k + 1)], xf_n[:, k, :], ident), marks + [nd])
            fst["xf_n"] = [tok]
            xt = run("vector", lambda e, ps=ps: e.tensor_scalar(xf_T[:, :], ps[:, 0:BANK], vecs[s][:, 0:1], vecs[s][:, 1:2],
                                                                ALU.mult, ALU.add), [tok, W[l]] + fst["xf_T"])
            give(i, xt)
            yield
            for c, n in enumerate(ff_rows):
                i, ps, marks = take()
                for m in range(2):
                    at = m * ff + P * c
                    tok = run("tensor", lambda e, ps=ps, m=m, at=at, n=n: e.matmul(
                        ps[0:n, BANK * m:BANK * (m + 1)], w_1[s][:, at:at + n], xf_T[:, :], start=True, stop=True),
                        marks + [xt, W[l]])
                nf = len(ff_rows)
                ge = run("scalar", lambda e, ps=ps, n=n, c=c: e.activation(
                    gel[0:n, :], ps[0:n, BANK:PAIR], ACT.Gelu, bias=vecs[s][0:n, 2 + nf + c:3 + nf + c]), [tok, W[l]] + fst["gel"])
                u = run("vector", lambda e, ps=ps, n=n, c=c: e.scalar_tensor_tensor(
                    out=uT[0:n, c, :], in0=ps[0:n, 0:BANK], scalar=vecs[s][0:n, 2 + c:3 + c], in1=gel[0:n, :],
                    op0=ALU.add, op1=ALU.mult), [ge] + fst["uT"])
                fst["gel"] = [u]
                give(i, u)
            fst["xf_T"] = [tok]
            yield
            i, ps, marks = take()
            for k in range(GROUP):
                for c, n in enumerate(ff_rows):
                    tok = run("tensor", lambda e, ps=ps, k=k, c=c, n=n: e.matmul(
                        ps[:, P * k:P * (k + 1)], uT[0:n, c, P * k:P * (k + 1)], w_2[s][0:n, c, :], start=c == 0,
                        stop=c == len(ff_rows) - 1), marks + [u])
            fst["uT"] = [tok]
            t0 = b * tiles + half * GROUP
            xg = X[:, t0:t0 + GROUP, :]
            add = run("vector", lambda e, ps=ps: e.tensor_tensor(xg, ps[:, 0:BANK].rearrange("p (t d) -> p t d", d=P), xg, ALU.add),
                      [tok])
            give(i, add)
            add = run("vector", lambda e: e.tensor_tensor(xg, xg, b2_all[s][:, :].unsqueeze(1).to_broadcast([P, GROUP, P]), ALU.add))
            for k in range(GROUP):
                x_ready[t0 + k] = add
            layer_end[l] = [tok, add]

        halves = tiles // GROUP
        xs_free = [[], []]
        load_layer(0)
        ff_jobs = []
        tail = []

        def advance(n=1):
            for _ in range(n):
                for g in list(tail):
                    if next(g, "end") == "end":
                        tail.remove(g)

        for l in range(layers):
            for b in range(batches):
                for half in range(halves):
                    if b == 0 and half == 0:
                        qkv_ready, tabs_ready = load_qkv(l)
                        if l + 1 < layers:
                            load_layer(l + 1)
                    xs_ready = shifted(xsT[b], b, half, [], xs_free[b] + used["qkv"])
                    for k in range(GROUP):
                        for _ in attention_tile(l, b, half * GROUP + k, qkv_ready, tabs_ready, xs_ready):
                            pass
                    for _ in feed_forward(l, b, half):
                        pass

        stores = []
        for t in range(all_tiles):
            fin = run("vector", lambda e, t=t: e.tensor_tensor(YA[:, t, :], X[:, t, :], YA[:, t, :], ALU.add), [ya_loaded, x_ready[t]])
        stores.append(load("out", out.rearrange("b (t p) d -> p (b t) d", p=P), YA[:, :, :], [fin]))
        prog.wait("sync", stores + [ya_stored])
        with nc.Block() as block:
            prog.emit(block)


NAMES = {"L0_attn_Wq": "Wq", "L0_attn_Wk": "Wk", "L0_attn_Wv": "Wv", "L0_attn_W_O": "W_O", "L0_ffn_Wqkv": "Wqkv",
         "L0_ffn_q_scale": "q_scale", "L0_ffn_k_scale": "k_scale", "L0_ffn_Wo": "Wo", "L0_ffn_ln_g": "ln_g",
         "L0_ffn_ln_b": "ln_b", "L0_ffn_W1": "W1", "L0_ffn_b1": "b1", "L0_ffn_W2": "W2", "L0_ffn_b2": "b2",
         "L0_attn_x": "x"}


def kernel(**inputs):
    import concourse.bacc as bacc
    from concourse.bass_utils import run_bass_kernel_spmd

    nc = bacc.Bacc("TRN2", target_bir_lowering=False, num_devices=1)
    arrays = {short: np.ascontiguousarray(inputs[name]) for name, short in NAMES.items()}
    shape = arrays["x"].shape
    arrays["consts"] = mask_constants()
    arrays["tab_c"], arrays["tab_s"] = rotary_constants(shape[1])
    ins = {n: nc.dram_tensor(n, a.shape, mybir.dt.from_np(a.dtype), kind="ExternalInput").ap() for n, a in arrays.items()}
    out = nc.dram_tensor("out", shape, F32, kind="ExternalOutput").ap()
    scratch = nc.dram_tensor("scratch", shape, F32, kind="Internal").ap()
    build(nc, ins, out, scratch)
    result = run_bass_kernel_spmd(nc, [arrays], core_ids=[0])
    return result.results[0]["out"]
```

```python
from contextlib import ExitStack

import numpy as np

import concourse.bass as bass
from concourse import mybir

F32 = mybir.dt.float32
BF16 = mybir.dt.bfloat16
I32 = mybir.dt.int32
ALU = mybir.AluOpType
ACT = mybir.ActivationFunctionType
AX_X = mybir.AxisListType.X

P = 128
BANK = 512
PAIR = 2 * BANK
EPS = 1e-5
NORM_FLOOR = 1e-12
MASKED = -1e30
RSQRT_MAGIC = float(0x5F3759DF)

A_HEADS = 16
A_DIM = 8
A_SLOT = 32
A_PER_GROUP = P // A_SLOT
A_GROUPS = A_HEADS // A_PER_GROUP

HEADS = 16
HEAD_DIM = 64
HALF = HEAD_DIM // 2
WINDOW = 32
SIM_SCALE = 8.0
INNER = HEADS * HEAD_DIM
CHUNKS = INNER // P
WPT = P // WINDOW
GROUP = 4


def rotary_constants(n):
    f = np.float32
    half = np.arange(0, HEAD_DIM, 2, dtype=f)
    inv_freq = f(1.0) / np.power(f(10000.0), half / f(HEAD_DIM)).astype(f)
    t = np.arange(n, dtype=f)
    freqs = (t[:, None] * inv_freq[None, :]).astype(f)
    base = (half + f(0.4 * HEAD_DIM)) / f(1.4 * HEAD_DIM)
    power = (t - f(n // 2)) / f(WINDOW // 2)
    scale = np.power(base[None, :], power[:, None]).astype(f)
    cos, sin = np.cos(freqs), np.sin(freqs)
    tab_c = np.zeros((n, 2, HEAD_DIM), f)
    tab_s = np.zeros((n, 2, HEAD_DIM), f)
    for m, s in enumerate((scale, f(1.0) / scale)):
        tab_c[:, m, :HALF] = tab_c[:, m, HALF:] = cos * s
        tab_s[:, m, :HALF] = -sin * s
        tab_s[:, m, HALF:] = sin * s
    return tab_c, tab_s


def mask_constants():
    i = np.arange(P)
    ident = np.eye(P, dtype=np.float32)
    rows = np.where(i[None, :] <= i[:, None], 0.0, MASKED).astype(np.float32)
    r = (i % WINDOW)[:, None]
    k = np.arange(2 * WINDOW)[None, :]
    win = np.where((k >= r) & (k <= r + WINDOW), 0.0, MASKED).astype(np.float32)
    win0 = win.copy()
    win0[:WINDOW, :WINDOW] = MASKED
    return np.concatenate([ident, rows, rows.T, win, win0], axis=1)


class Program:

    def __init__(self, nc, ctx):
        self.nc, self.ctx = nc, ctx
        self.queues = {e: [] for e in ("tensor", "vector", "scalar", "gpsimd", "sync")}
        self.done = {e: ctx.enter_context(nc.semaphore(f"{e}_done")) for e in ("tensor", "vector", "scalar", "gpsimd")}
        self.count = {e: 0 for e in self.done}
        self.seen = {e: {} for e in self.queues}
        self.dma = {}

    def wait(self, engine, marks):
        for key, sem, value in marks:
            if self.seen[engine].get(key, 0) < value:
                self.seen[engine][key] = value
                self.queues[engine].append(lambda e, sem=sem, value=value: e.wait_ge(sem, value))

    def run(self, engine, instruction, after=(), mark=True):
        self.wait(engine, after)
        if engine != "tensor" and self.count[engine]:
            self.wait(engine, [(engine, self.done[engine], self.count[engine])])
        if not mark:
            self.queues[engine].append(instruction)
            return None
        self.count[engine] += 1
        sem = self.done[engine]
        self.queues[engine].append(lambda e: instruction(e).then_inc(sem, 1))
        return (engine, sem, self.count[engine])

    def load(self, stream, out, in_, after=(), engine="sync"):
        if stream not in self.dma:
            self.dma[stream] = [self.ctx.enter_context(self.nc.semaphore(f"dma_{stream}")), 0]
        entry = self.dma[stream]
        entry[1] += 16
        sem = entry[0]
        self.wait(engine, after)
        self.queues[engine].append(lambda e: e.dma_start(out, in_).then_inc(sem, 16))
        return (f"dma_{stream}", sem, entry[1])

    def emit(self, block):
        for name in self.queues:
            def body(engine, queue=self.queues[name]):
                for instruction in queue:
                    instruction(engine)
            {"tensor": block.tensor, "vector": block.vector, "scalar": block.scalar,
             "gpsimd": block.gpsimd, "sync": block.sync}[name](body)


def build(nc, ins, out, scratch, parts_dram):
    x, consts, tab_c, tab_s = ins["x"], ins["consts"], ins["tab_c"], ins["tab_s"]
    batches, seq, dim = x.shape
    layers = ins["Wqkv"].shape[0]
    tiles = seq // P
    all_tiles = batches * tiles
    ff = ins["W2"].shape[1]
    ff_rows = [min(P, ff - P * c) for c in range((ff + P - 1) // P)]
    assert dim == P and ins["Wqkv"].shape[2] == 3 * INNER

    with ExitStack() as ctx:
        prog = Program(nc, ctx)
        run, load = prog.run, prog.load

        def sb(name, shape, dt=F32):
            return ctx.enter_context(nc.sbuf_tensor(name, shape, dt))

        banks = ctx.enter_context(nc.psum_tensor("banks", [P, 4, PAIR], F32))
        free_pairs = [(i, []) for i in range(4)]

        def take():
            i, marks = free_pairs.pop(0)
            return i, banks[:, i, :], marks

        def give(i, *marks):
            free_pairs.append((i, list(marks)))

        ARENA = 37 * PAIR + 8
        arena = sb("arena", [P, ARENA])
        used_words = {"A": 0, "stack": 0}

        def carve(owner, words):
            at = used_words[owner]
            used_words[owner] = at + words
            assert used_words[owner] <= ARENA
            return arena[:, at:at + words]

        ident = sb("ident", [P, P])[:, :]
        cst_b = sb("cst_b", [P, 3 * P + 4 * WINDOW], BF16)
        ident_b = cst_b[:, 0:P]
        mask_rows, mask_cols = cst_b[:, P:2 * P], cst_b[:, 2 * P:3 * P]
        win_b = sb("win_b", [P, 2, 8, 2 * WINDOW], BF16)
        base_c, base_s = sb("base_c", [P, tiles, 2, HEAD_DIM]), sb("base_s", [P, tiles, 2, HEAD_DIM])
        ident_loaded = load("const", ident, consts[:, 0:P])
        X = sb("X", [P, all_tiles, P])
        x_loaded = load("x", X[:, :, :], x.rearrange("b (t p) d -> p (b t) d", p=P))
        for tab, src in ((base_c, tab_c), (base_s, tab_s)):
            tabs_loaded = load("tabs", tab[:, :, :, :], src.rearrange("(t p) m d -> p t m d", p=P))
        cst = carve("A", 3 * P + 4 * WINDOW)
        cst_loaded = load("masks", cst, consts)
        c_ready = run("vector", lambda e: e.tensor_copy(cst_b[:, :], cst), [cst_loaded])
        for m in range(2):
            at = 3 * P + 2 * WINDOW * m
            c_ready = run("vector", lambda e, m=m, at=at: e.tensor_copy(
                win_b[:, m, :, :], cst_b[:, at:at + 2 * WINDOW].unsqueeze(1).to_broadcast([P, 8, 2 * WINDOW])))

        RS = 2 * HEADS
        rs_h, rs_t = sb("rs_h", [P, RS], I32), sb("rs_t", [P, RS])

        def rsqrt(y, v, n, after=()):
            h, t = rs_h[:, 0:n], rs_t[:, 0:n]
            run("vector", lambda e: e.tensor_scalar(h, v.bitcast(I32), 1, None, ALU.logical_shift_right), after)
            run("vector", lambda e: e.tensor_scalar(y.bitcast(I32), h, -1.0, RSQRT_MAGIC, ALU.mult, ALU.add))
            for _ in range(3):
                run("vector", lambda e: e.tensor_tensor(t, y, y, ALU.mult))
                run("vector", lambda e: e.scalar_tensor_tensor(out=t, in0=t, scalar=-0.5, in1=v, op0=ALU.mult, op1=ALU.mult))
                last = run("vector", lambda e: e.scalar_tensor_tensor(out=y, in0=t, scalar=1.5, in1=y, op0=ALU.add, op1=ALU.mult))
            return last

        stats = sb("stats", [P, 6])
        mean_var = sb("mean_var", [P, all_tiles, 2])
        ln_v, ln_r = sb("ln_v", [P, all_tiles]), sb("ln_r", [P, all_tiles])

        def norm_tiles(src, dst, n, after):
            for i in range(n):
                run("vector", lambda e, i=i: e.bn_stats(stats[:, :], src[:, i, :]), after if i == 0 else ())
                run("vector", lambda e, i=i: e.bn_aggr(mean_var[:, i, :], stats[:, :]))
            run("vector", lambda e: e.tensor_scalar(ln_v[:, 0:n], mean_var[:, 0:n, 1], EPS, None, ALU.add))
            rsqrt(ln_r[:, 0:n], ln_v[:, 0:n], n)
            for i in range(n):
                last = run("vector", lambda e, i=i: e.tensor_scalar(
                    dst[:, i, :], src[:, i, :], mean_var[:, i, 0:1], ln_r[:, i:i + 1], ALU.subtract, ALU.mult))
            return last

        x_ready = [norm_tiles(X, X, all_tiles, [x_loaded])] * all_tiles

        PARTS = 3
        ROWS = A_DIM * PARTS * PARTS
        RING = 3 * A_PER_GROUP
        QS = [carve("A", seq // 2).bitcast(BF16) for _ in range(RING)]
        KS = [carve("A", seq // 2).bitcast(BF16) for _ in range(RING)]
        w_diag = [carve("A", P) for m in range(2)]
        w_pad = carve("A", A_HEADS * A_SLOT).rearrange("p (h d) -> p h d", d=A_SLOT)
        w_out_a = carve("A", P)
        VA = carve("A", tiles * A_HEADS * A_SLOT).rearrange("p (t h d) -> p t h d", h=A_HEADS, d=A_SLOT)
        xnT = carve("A", seq)
        parts = carve("A", PARTS * seq // 2).bitcast(BF16).rearrange("p (s n) -> p s n", s=PARTS)
        rest = carve("A", seq)
        m_neg = [carve("A", tiles * A_PER_GROUP).rearrange("p (t j) -> p t j", j=A_PER_GROUP) for _ in range(2)]
        m_parts = [carve("A", PARTS * seq // 2).bitcast(BF16).rearrange("p (s n) -> p s n", s=PARTS) for _ in range(2)]
        m_rest = carve("A", seq)
        ones_b = carve("A", seq // 2).bitcast(BF16)
        pt_ring = [carve("A", seq) for _ in range(4)]
        accT = carve("A", seq)
        a_sum = carve("A", tiles * A_PER_GROUP).rearrange("p (t j) -> p t j", j=A_PER_GROUP)
        xa = carve("A", seq).rearrange("p (t d) -> p t d", d=P)
        ya = carve("A", seq).rearrange("p (t d) -> p t d", d=P)
        cat = carve("A", all_tiles * P).rearrange("p (t d) -> p t d", d=P)

        for buf in w_diag:
            zeroed = run("gpsimd", lambda e, buf=buf: e.memset(buf, 0.0))
        zeroed = run("gpsimd", lambda e: e.memset(w_pad, 0.0))
        ones_set = run("gpsimd", lambda e: e.memset(ones_b[0:PARTS, :], 1.0))
        for m, name in enumerate(("Wq", "Wk", "Wv")):
            for h in range(A_HEADS):
                rows = slice(A_DIM * h, A_DIM * (h + 1))
                dst = w_pad[rows, h, 0:A_DIM] if m == 2 else w_diag[m][rows, rows]
                w_loaded = load("w_a", dst, ins[name][h], [zeroed], engine=("sync", "scalar")[h % 2])
        wo_a_loaded = load("w_out_a", w_out_a, ins["W_O"])
        for s in range(RING):
            ones_stored = load("ones", KS[s][ROWS:ROWS + PARTS, :], ones_b[0:PARTS, :], [ones_set])

        def split(src, dst, spare, after, free):
            hi = run("scalar", lambda e: e.copy(dst[:, 0, :], src), after + free)
            v1 = run("vector", lambda e: e.tensor_tensor(spare, src, dst[:, 0, :], ALU.subtract), [hi])
            mid = run("scalar", lambda e: e.copy(dst[:, 1, :], spare), [v1])
            lo = run("vector", lambda e: e.tensor_tensor(dst[:, 2, :], spare, dst[:, 1, :], ALU.subtract), [mid])
            return v1, lo

        pt_free = [[], [], [], []]
        a_state = {"turn": 0, "xnT": [], "acc": [], "VA": [], "parts": []}
        stack_free = [[] for _ in range(RING)]
        stack_ready, row_ready, proj = {}, {}, {}

        def project(b):
            i, ps, marks = take()
            for t in range(tiles):
                tok = run("tensor", lambda e, ps=ps, t=t: e.transpose(ps[:, P * t:P * (t + 1)], X[:, b * tiles + t, :], ident),
                          marks + [ident_loaded, x_ready[b * tiles + t]])
            xnT_ready = run("scalar", lambda e, ps=ps: e.copy(xnT, ps), [tok] + a_state["xnT"])
            give(i, xnT_ready)
            for m in range(2):
                i, ps, marks = take()
                for c in range(seq // BANK):
                    tok = run("tensor", lambda e, ps=ps, m=m, c=c: e.matmul(
                        ps[:, BANK * c:BANK * (c + 1)], w_diag[m], xnT[:, BANK * c:BANK * (c + 1)], start=True, stop=True),
                        marks + [xnT_ready, w_loaded])
                v1, lo = split(ps, parts, rest, [tok], a_state["parts"])
                give(i, v1)
                proj[b, m] = load(f"parts{m}", parts_dram[b, m].rearrange("s p n -> p s n"), parts, [lo])
                a_state["parts"] = [proj[b, m]]
            yield

        def project_v(b):
            for t in range(tiles):
                i, ps, marks = take()
                tok = run("tensor", lambda e, ps=ps, t=t: e.matmul(
                    ps[:, 0:BANK], xnT[:, P * t:P * (t + 1)], w_pad.rearrange("p h d -> p (h d)"), start=True, stop=True), marks)
                va = run("scalar", lambda e, ps=ps, t=t: e.copy(VA[:, t, :, :].rearrange("p h d -> p (h d)"), ps[:, 0:BANK]),
                         [tok] + a_state["VA"])
                give(i, va)
            a_state["xnT"] = [tok]
            a_state["VA_ready"] = run("gpsimd", lambda e: e.memset(VA[:, :, :, A_DIM:A_DIM + 1], 1.0), [va])

        def load_stacks(b, g):
            for j in range(A_PER_GROUP):
                h = g * A_PER_GROUP + j
                slot = ((b * A_GROUPS + g) * A_PER_GROUP + j) % RING
                src = [parts_dram[b, m, :, A_DIM * h:A_DIM * (h + 1), :] for m in range(2)]
                for s in range(PARTS):
                    lo = s * PARTS * A_DIM
                    load(f"stack{slot}", QS[slot][lo:lo + PARTS * A_DIM, :],
                         src[0][s:s + 1].to_broadcast([PARTS, A_DIM, seq]), stack_free[slot] + [proj[b, 0]],
                         engine="sync")
                    done = load(f"stack{slot}", KS[slot][lo:lo + PARTS * A_DIM, :], src[1],
                                stack_free[slot] + [proj[b, 1]], engine="sync")
                stack_ready[b, g, j] = done

        def row_maxima(b, g):
            n_g = b * A_GROUPS + g
            mn, mp = m_neg[n_g % 2], m_parts[n_g % 2]
            slots = [(n_g * A_PER_GROUP + j) % RING for j in range(A_PER_GROUP)]
            for qt in range(tiles):
                n = P * (qt + 1)
                for j, slot in enumerate(slots):
                    i, ps, marks = take()
                    for c in range((n + BANK - 1) // BANK):
                        e1 = min(n, BANK * (c + 1))
                        run("tensor", lambda e, ps=ps, slot=slot, qt=qt, c=c, e1=e1: e.matmul(
                            ps[:, BANK * c:e1], QS[slot][0:ROWS, P * qt:P * (qt + 1)], KS[slot][0:ROWS, BANK * c:e1],
                            start=True, stop=True), marks + [stack_ready[b, g, j]], mark=False)
                    tok = run("tensor", lambda e, ps=ps, n=n: e.matmul(
                        ps[:, n - P:n], ident_b, mask_rows, start=False, stop=True, skip_group_check=True), [c_ready])
                    mx = run("vector", lambda e, ps=ps, n=n, qt=qt, j=j: e.tensor_reduce(
                        mn[:, qt, j:j + 1], ps[:, 0:n], AX_X, ALU.max, negate=True), [tok])
                    give(i, mx)
                yield
            i, ps, marks = take()
            for t in range(tiles):
                tok = run("tensor", lambda e, ps=ps, t=t: e.transpose(ps[0:A_PER_GROUP, P * t:P * (t + 1)], mn[:, t, :], ident),
                          marks + [mx])
            rows4 = slice(0, A_PER_GROUP)
            v1, lo = split(ps[rows4], mp[rows4], m_rest[rows4], [tok], a_state.get(("mp", n_g % 2), []))
            give(i, v1)
            for j, slot in enumerate(slots):
                for s in range(PARTS):
                    row_ready[b, g, j] = load(f"rows{slot}", QS[slot][ROWS + s:ROWS + s + 1, :], mp[j:j + 1, s, :], [lo])
            a_state["mp", n_g % 2] = [row_ready[b, g, j] for j in range(A_PER_GROUP)]
            yield

        def weigh(b, g):
            acc_i, acc, acc_marks = take()
            for kt in range(tiles):
                q0 = P * kt
                for j in range(A_PER_GROUP):
                    slot = ((b * A_GROUPS + g) * A_PER_GROUP + j) % RING
                    h = g * A_PER_GROUP + j
                    i, ps, marks = take()
                    spans = [(max(q0, BANK * c), BANK * (c + 1)) for c in range(seq // BANK) if q0 < BANK * (c + 1)]
                    for s0, s1 in spans:
                        tok = run("tensor", lambda e, ps=ps, slot=slot, kt=kt, s0=s0, s1=s1: e.matmul(
                            ps[:, s0:s1], KS[slot][0:ROWS + PARTS, P * kt:P * (kt + 1)], QS[slot][0:ROWS + PARTS, s0:s1],
                            start=True, stop=True), marks + [row_ready[b, g, j], ones_stored])
                        if s0 == q0:
                            tok = run("tensor", lambda e, ps=ps, q0=q0: e.matmul(
                                ps[:, q0:q0 + P], ident_b, mask_cols, start=False, stop=True, skip_group_check=True))
                    if kt == tiles - 1:
                        stack_free[slot] = [tok]
                    turn = a_state["turn"]
                    buf, was = pt_ring[turn], pt_free[turn]
                    ex = run("scalar", lambda e, ps=ps, buf=buf, q0=q0: e.activation(
                        buf[:, q0:seq], ps[:, q0:seq], ACT.Exp, scale=float(A_DIM) ** -0.5), [tok] + was)
                    give(i, ex)
                    late.append((j, kt, h, buf, spans, ex, turn))
                    a_state["turn"] = (turn + 1) % 4
                    if len(late) > 2:
                        gather(acc, acc_marks, *late.pop(0))
                yield
            while late:
                gather(acc, acc_marks, *late.pop(0))
            tok = a_state["gathered"]
            at = run("scalar", lambda e: e.copy(accT, acc), [tok] + a_state["acc"])
            give(acc_i, at)
            i, ps, marks = take()
            for t in range(tiles):
                tok = run("tensor", lambda e, ps=ps, t=t: e.transpose(ps[:, P * t:P * (t + 1)], accT[:, P * t:P * (t + 1)], ident),
                          marks + [at])
            a_state["acc"] = [tok]
            psv = ps.rearrange("p (t j c) -> p t j c", j=A_PER_GROUP, c=A_SLOT)
            run("vector", lambda e: e.reciprocal(a_sum, psv[:, :, :, A_DIM]), [tok])
            last = run("vector", lambda e: e.tensor_tensor(
                cat[:, b * tiles:(b + 1) * tiles, :].rearrange("p t (g j d) -> p t g j d", j=A_PER_GROUP, d=A_DIM)[:, :, g],
                psv[:, :, :, 0:A_DIM], a_sum.unsqueeze(3).to_broadcast([P, tiles, A_PER_GROUP, A_DIM]), ALU.mult))
            give(i, last)
            a_state["VA"] = [tok]
            a_state["cat"] = last
            yield

        late = []

        def gather(acc, acc_marks, j, kt, h, buf, spans, ex, turn):
            for s0, s1 in spans:
                tok = run("tensor", lambda e, s0=s0, s1=s1: e.matmul(
                    acc[A_SLOT * j:A_SLOT * (j + 1), s0:s1], VA[:, kt, h, :], buf[:, s0:s1],
                    start=kt == 0, stop=True, skip_group_check=True), acc_marks + [ex, a_state["VA_ready"]])
            pt_free[turn] = [tok]
            a_state["gathered"] = tok

        def output_a(b):
            was = a_state.get("ya", [])
            xa_loaded = load("xa", xa, x[b].rearrange("(e t) d -> e t d", t=tiles), was)
            i, ps, marks = take()
            for t in range(tiles):
                tok = run("tensor", lambda e, ps=ps, t=t: e.matmul(
                    ps[:, P * t:P * (t + 1)], cat[:, b * tiles + t, :], w_out_a, start=True, stop=True),
                    marks + [a_state["cat"], wo_a_loaded])
            y_ready = run("vector", lambda e, ps=ps: e.tensor_tensor(
                ya.rearrange("p t d -> p (t d)"), ps, xa.rearrange("p t d -> p (t d)"), ALU.add), [tok, xa_loaded] + was)
            give(i, y_ready)
            a_state["ya"] = [load("ya", scratch[b].rearrange("(e t) d -> e t d", t=tiles), ya, [y_ready]), y_ready]
            a_state["end"] = [tok, y_ready, a_state["ya"][0]]

        def in_turn(*jobs):
            jobs = list(jobs)
            while jobs:
                jobs = [j for j in jobs if next(j, "end") != "end"]

        order = [(b, g) for b in range(batches) for g in range(A_GROUPS)]
        for _ in project(0):
            pass
        load_stacks(0, 0)
        load_stacks(0, 1)
        in_turn(row_maxima(0, 0))
        project_v(0)
        for n_g, (b, g) in enumerate(order):
            jobs = [weigh(b, g)]
            if g == A_GROUPS - 2 and b + 1 < batches:
                jobs.append(project(b + 1))
            if n_g + 1 < len(order):
                jobs.append(row_maxima(*order[n_g + 1]))
            in_turn(*jobs)
            if n_g + 2 < len(order):
                load_stacks(*order[n_g + 2])
            if g == A_GROUPS - 1:
                output_a(b)
                if b + 1 < batches:
                    project_v(b + 1)
        was_a = a_state["end"]

        def stack(*shape):
            flat = carve("stack", int(np.prod(shape)))
            names = " ".join("abc"[:len(shape)])
            return flat.rearrange(f"p ({names}) -> p {names}", **{k: v for k, v in zip("abc", shape)}) if len(shape) > 1 else flat

        w_qkv = sb("w_qkv", [P, 3 * INNER])
        w_o = [sb(f"w_o{s}", [P, CHUNKS, P]) for s in range(2)]
        w_1 = [sb(f"w_1{s}", [P, 2 * ff]) for s in range(2)]
        w_2 = [sb(f"w_2{s}", [P, len(ff_rows), P]) for s in range(2)]
        vecs = [sb(f"vecs{s}", [P, 2 + 2 * len(ff_rows)]) for s in range(2)]
        b2_all = [sb(f"b2_all{s}", [P, P]) for s in range(2)]
        qk_gain = sb("qk_gain", [P, 2, HEAD_DIM])
        tab_cl, tab_sl = sb("tab_cl", [P, tiles, 2, HEAD_DIM]), sb("tab_sl", [P, tiles, 2, HEAD_DIM])
        qk_raw = [stack(2, INNER) for _ in range(2)]
        qk_sq, qk_sw, qk_rot = stack(2, INNER), stack(2, INNER), stack(2, INNER)
        PTs = [stack(2 * HEADS, P).rearrange("p (s h) q -> p s h q", s=2) for _ in range(2)]
        PBT = stack(2 * INNER // 2)
        xsT = [stack(seq + 1) for b in range(batches)]
        xfT = [stack(seq + 1) for b in range(batches)]
        QT = stack(CHUNKS, P)
        KT = [stack(CHUNKS, WINDOW + P) for s in range(2)]
        V = [stack(INNER) for s in range(3)]
        Vp = [stack(INNER) for s in range(3)]
        PB = stack(HEADS, 2 * WINDOW)
        ss, rn = sb("ss", [P, 2 * HEADS]), sb("rn", [P, 2 * HEADS])
        mx_t, sm_t, rs_o = sb("mx_t", [P, HEADS]), sb("sm_t", [P, HEADS]), sb("rs_o", [P, HEADS])
        OT = stack(CHUNKS, P)
        xf_n, xf_T = stack(GROUP, P), stack(GROUP * P)
        gel, uT = xf_n.rearrange("p t d -> p (t d)"), stack(len(ff_rows), GROUP * P)

        m0 = run("gpsimd", lambda e: e.memset(PTs[0], 0.0), was_a)
        m0 = run("gpsimd", lambda e: e.memset(PTs[1], 0.0))
        for b in range(batches):
            for buf in (xsT[b], xfT[b]):
                m0 = run("gpsimd", lambda e, buf=buf: e.memset(buf[HEAD_DIM:P, 0:1], 0.0))
        zero_ready = m0

        W = {}
        layer_end = {}
        used = {"qk": [], "v": [], "tabs": []}

        def load_layer(l):
            s = l % 2
            free = layer_end.get(l - 2, [])
            load(f"w{s}", w_o[s][:, :, :], ins["Wo"][l].rearrange("(c p) d -> p c d", p=P), free)
            load(f"w{s}", w_1[s][:, :], ins["W1"][l])
            for c, n in enumerate(ff_rows):
                load(f"w{s}", w_2[s][0:n, c, :], ins["W2"][l, P * c:P * c + n, :])
                for m in range(2):
                    at = m * ff + P * c
                    load(f"w{s}", vecs[s][0:n, 2 + m * len(ff_rows) + c:3 + m * len(ff_rows) + c],
                         ins["b1"][l, at:at + n].rearrange("(p a) -> p a", a=1))
            load(f"w{s}", vecs[s][:, 0:1], ins["ln_g"][l].rearrange("(p a) -> p a", a=1))
            load(f"w{s}", vecs[s][:, 1:2], ins["ln_b"][l].rearrange("(p a) -> p a", a=1))
            W[l] = load(f"w{s}", b2_all[s][:, :], ins["b2"][l:l + 1, :].to_broadcast([P, P]))

        def load_qkv(l):
            ready = {"qk": load("w_qk", w_qkv[:, 0:2 * INNER], ins["Wqkv"][l, :, 0:2 * INNER], used["qk"])}
            return ready

        def load_tables(l, ready):
            load("gain", qk_gain[:, 0, :], ins["q_scale"][l:l + 1, :].to_broadcast([P, HEAD_DIM]), used["tabs"])
            gain = load("gain", qk_gain[:, 1, :], ins["k_scale"][l:l + 1, :].to_broadcast([P, HEAD_DIM]))
            g = qk_gain[:, :, :].unsqueeze(1).to_broadcast([P, tiles, 2, HEAD_DIM])
            run("gpsimd", lambda e: e.tensor_tensor(tab_cl[:, :, :, :], base_c[:, :, :, :], g, ALU.mult), [gain, tabs_loaded] + used["tabs"])
            for d, s in ((0, HALF), (HALF, 0)):
                gs = qk_gain[:, :, s:s + HALF].unsqueeze(1).to_broadcast([P, tiles, 2, HALF])
                tabs = run("gpsimd", lambda e, d=d, gs=gs: e.tensor_tensor(
                    tab_sl[:, :, :, d:d + HALF], base_s[:, :, :, d:d + HALF], gs, ALU.mult))
            ready["tabs"] = tabs

        def shifted(dst, b, half, after, free):
            i, ps, marks = take()
            for k in range(GROUP):
                t = b * tiles + half * GROUP + k
                tok = run("tensor", lambda e, ps=ps, k=k, t=t: e.transpose(ps[:, P * k:P * (k + 1)], X[:, t, :], ident),
                          marks + [x_ready[t]] + after)
            c0 = half * GROUP * P
            run("scalar", lambda e: e.copy(dst[0:64, c0:c0 + GROUP * P], ps[0:64, 0:GROUP * P]), [tok, zero_ready] + free)
            done = run("scalar", lambda e: e.copy(dst[64:P, c0 + 1:c0 + 1 + GROUP * P], ps[64:P, 0:GROUP * P]))
            give(i, done)
            return done

        st = {"V": [was_a] * 3, "Vp": [was_a] * 3, "KT": [was_a] * 2, "KTready": [None, None],
              "raw": [was_a] * len(qk_raw), "sq": was_a, "sw": was_a, "PBT": was_a, "rot0": was_a, "rot1": was_a, "PT": [was_a] * 2, "PB": was_a, "QT": was_a, "ON": was_a, "OT": was_a,
              "n": 0}

        def attention_tile(l, b, t, ready, xs_ready):
            n = st["n"]
            st["n"] += 1
            s = l % 2
            first = t == 0
            lhs = xsT[b][:, P * t:P * (t + 1)]
            raw, rot = qk_raw[n % len(qk_raw)], qk_rot
            for m in range(2):
                i, ps, marks = take()
                for c in range(2):
                    at = m * INNER + BANK * c
                    tok = run("tensor", lambda e, ps=ps, c=c, at=at: e.matmul(
                        ps[:, BANK * c:BANK * (c + 1)], lhs, w_qkv[:, at:at + BANK], start=True, stop=True),
                        marks + [ready["qk"], xs_ready])
                run("scalar", lambda e, ps=ps, m=m: e.copy(raw[:, m, :], ps), [tok] + st["raw"][n % len(qk_raw)])
                sq = run("scalar", lambda e, ps=ps, m=m: e.activation(qk_sq[:, m, :], ps, ACT.Square), st["sq"])
                give(i, sq)
            used["qk"] = [tok]
            yield
            def heads(a):
                return a.rearrange("p m (h d) -> p (m h) d", d=HEAD_DIM)

            rd = run("vector", lambda e: e.tensor_reduce(ss[:, :], heads(qk_sq), AX_X, ALU.add), [sq])
            st["sq"] = [rd]
            run("vector", lambda e: e.tensor_scalar(ss[:, :], ss[:, :], NORM_FLOOR ** 2, None, ALU.max))
            rsqrt(rn[:, :], ss[:, :], 2 * HEADS)
            for m in range(2):
                qn = run("vector", lambda e, m=m: e.tensor_tensor(
                    raw[:, m, :].rearrange("p (h d) -> p h d", d=HEAD_DIM), raw[:, m, :].rearrange("p (h d) -> p h d", d=HEAD_DIM),
                    rn[:, HEADS * m:HEADS * (m + 1)].unsqueeze(2).to_broadcast([P, HEADS, HEAD_DIM]), ALU.mult))
                for d, o in ((0, HALF), (HALF, 0)):
                    src = raw[:, m, :].rearrange("p (h d) -> p h d", d=HEAD_DIM)[:, :, o:o + HALF]
                    dst = qk_sw[:, m, :].rearrange("p (h d) -> p h d", d=HEAD_DIM)[:, :, d:d + HALF]
                    tb = tab_sl[:, t, m, d:d + HALF].unsqueeze(1).to_broadcast([P, HEADS, HALF])
                    sw = run("gpsimd", lambda e, dst=dst, src=src, tb=tb: e.tensor_tensor(dst, src, tb, ALU.mult),
                             [qn, ready["tabs"]] + st["sw"])
                st["swm"] = st.get("swm", {})
                st["swm"][m] = sw
            for m in range(2):
                rc = run("vector", lambda e, m=m: e.tensor_tensor(
                    rot[:, m, :].rearrange("p (h d) -> p h d", d=HEAD_DIM), raw[:, m, :].rearrange("p (h d) -> p h d", d=HEAD_DIM),
                    tab_cl[:, t, m, :].unsqueeze(1).to_broadcast([P, HEADS, HEAD_DIM]), ALU.mult),
                    [ready["tabs"]] + st["rot%d" % m])
            used["tabs"] = [sw, rc]
            st["raw"][n % len(qk_raw)] = [sw, rc]
            swm = dict(st["swm"])
            yield
            rotated = {m: run("vector", lambda e, m=m: e.tensor_tensor(rot[:, m, :], rot[:, m, :], qk_sw[:, m, :], ALU.add), [swm[m]])
                       for m in (1, 0)}
            st["sw"] = [rotated[0]]
            yield
            kt_buf = KT[n % 2]
            for m in (1, 0):
                i, ps, marks = take()
                for c in range(CHUNKS):
                    tok = run("tensor", lambda e, ps=ps, c=c, m=m: e.transpose(
                        ps[:, P * c:P * (c + 1)], rot[:, m, P * c:P * (c + 1)], ident), marks + [rotated[m]])
                st["rot%d" % m] = [tok]
                if m:
                    k_ready = run("scalar", lambda e, ps=ps: e.copy(
                        kt_buf[:, :, WINDOW:WINDOW + P], ps.rearrange("p (c q) -> p c q", q=P)), [tok] + st["KT"][n % 2])
                    give(i, k_ready)
                else:
                    q_ready = run("scalar", lambda e, ps=ps: e.copy(QT.rearrange("p c q -> p (c q)"), ps), [tok] + st["QT"])
                    give(i, q_ready)
            if first:
                kp = run("gpsimd", lambda e: e.memset(kt_buf[:, :, 0:WINDOW], 0.0), st["KT"][n % 2])
            else:
                before = KT[(n - 1) % 2]
                kp = run("gpsimd", lambda e: e.tensor_copy(kt_buf[:, :, 0:WINDOW], before[:, :, P:P + WINDOW]),
                         st["KT"][n % 2] + [st["KTready"][(n - 1) % 2]])
            st["KTready"][n % 2] = k_ready
            yield
            i, ps, marks = take()
            for half in range(2):
                run("tensor", lambda e, ps=ps, half=half: e.matmul(
                    ps[:, BANK * half:BANK * (half + 1)], ident_b, win_b[:, int(first), :, :].rearrange("p c k -> p (c k)"),
                    start=True, stop=True), marks + [c_ready], mark=False)
            for c in range(CHUNKS):
                for half in range(2):
                    for w in range(WPT):
                        r = slice(64 * half, 64 * half + 64)
                        col = BANK * half + 2 * WINDOW * c
                        tok = run("tensor", lambda e, ps=ps, r=r, c=c, w=w, col=col: e.matmul(
                            ps[WINDOW * w:WINDOW * (w + 1), col:col + 2 * WINDOW], QT[r, c, WINDOW * w:WINDOW * (w + 1)],
                            kt_buf[r, c, WINDOW * w:WINDOW * (w + 2)], start=False, stop=True, skip_group_check=True),
                            [q_ready, k_ready, kp], mark=c == CHUNKS - 1 and w == WPT - 1 and half == 1)
            st["QT"] = [tok]
            st["KT"][n % 2] = [tok]
            st["KT"][(n - 1) % 2] = st["KT"][(n - 1) % 2] + [kp]
            sc = ps.rearrange("p (h k) -> p h k", k=2 * WINDOW)
            run("vector", lambda e: e.tensor_reduce(mx_t[:, :], sc, AX_X, ALU.max), [tok])
            sub = run("vector", lambda e: e.tensor_tensor(PB, sc, mx_t[:, :].unsqueeze(2).to_broadcast([P, HEADS, 2 * WINDOW]),
                                                          ALU.subtract), st["PB"])
            give(i, sub)
            i, ps, marks = take()
            for c in range(2):
                at = 2 * INNER + BANK * c
                tok = run("tensor", lambda e, ps=ps, c=c, at=at: e.matmul(
                    ps[:, BANK * c:BANK * (c + 1)], lhs, w_qkv[:, at:at + BANK], start=True, stop=True), marks + [ready["v"]])
            used["v"] = [tok]
            v, vp = V[n % 3], Vp[n % 3]
            v_ready = run("scalar", lambda e, ps=ps: e.copy(v, ps), [tok] + st["V"][n % 3])
            give(i, v_ready)
            if first:
                vp_marks = [run("gpsimd", lambda e: e.memset(vp[0:WINDOW, :], 0.0), st["Vp"][n % 3])]
            else:
                prev = V[(n - 1) % 3]
                vp_marks = [load(f"vp_head{n % 3}", vp[0:WINDOW, :], prev[P - WINDOW:P, :], st["Vp"][n % 3])]
            vp_marks.append(load(f"vp_body{n % 3}", vp[WINDOW:P, :], v[0:P - WINDOW, :], [v_ready] + st["Vp"][n % 3]))
            st["V"][n % 3] = [vp_marks[-1]]
            if not first:
                st["V"][(n - 1) % 3] = st["V"][(n - 1) % 3] + [vp_marks[0]]
            yield
            ex = run("scalar", lambda e: e.activation(PB, PB, ACT.Exp, scale=SIM_SCALE), [sub])
            yield
            run("vector", lambda e: e.tensor_reduce(sm_t[:, :], PB, AX_X, ALU.add), [ex])
            run("vector", lambda e: e.reciprocal(rs_o[:, :], sm_t[:, :]))
            run("vector", lambda e: e.tensor_tensor(PB, PB, rs_o[:, :].unsqueeze(2).to_broadcast([P, HEADS, 2 * WINDOW]), ALU.mult))
            bt = run("vector", lambda e: e.transpose(PBT, PB), st["PBT"])
            st["PB"] = [bt]
            yield
            PT = PTs[n % 2]
            for w in range(WPT):
                r = slice(WINDOW * w, WINDOW * (w + 1))
                pt = run("scalar", lambda e, r=r: e.copy(
                    PT[r, :, :, r].rearrange("p s h q -> p h s q"), PBT.rearrange("p (h s q) -> p h s q", s=2, q=WINDOW)[r]),
                    [bt, zero_ready] + st["PT"][n % 2])
            st["PBT"] = [pt]
            yield
            i, ps, marks = take()
            for c in range(CHUNKS):
                for src, prior in ((v, 0), (vp, 1)):
                    for half in range(2):
                        hh = half * CHUNKS + c
                        vs = slice(HEAD_DIM * (2 * c + half), HEAD_DIM * (2 * c + half + 1))
                        tok = run("tensor", lambda e, ps=ps, c=c, src=src, prior=prior, half=half, hh=hh, vs=vs: e.matmul(
                            ps[64 * half:64 * half + 64, P * c:P * (c + 1)], src[:, vs], PT[:, 1 - prior, hh, :],
                            start=not prior, stop=bool(prior)), marks + [pt, v_ready] + vp_marks, mark=c == CHUNKS - 1)
            st["PT"][n % 2] = [tok]
            st["V"][n % 3] = st["V"][n % 3] + [tok]
            st["Vp"][n % 3] = [tok]
            ot = run("scalar", lambda e, ps=ps: e.copy(OT.rearrange("p c q -> p (c q)"), ps), [tok] + st["OT"])
            give(i, ot)
            yield
            i, ps, marks = take()
            for c in range(CHUNKS):
                tok = run("tensor", lambda e, ps=ps, c=c: e.matmul(ps[:, 0:P], OT[:, c, :], w_o[s][:, c, :], start=c == 0,
                                                                   stop=c == CHUNKS - 1), marks + [ot, W[l]])
            st["OT"] = [tok]
            x_ready[b * tiles + t] = run("vector", lambda e, ps=ps: e.tensor_tensor(
                X[:, b * tiles + t, :], ps[:, 0:P], X[:, b * tiles + t, :], ALU.add), [tok])
            give(i, x_ready[b * tiles + t])

        fst = {"xfT": [was_a] * 2, "xf_n": was_a, "xf_T": was_a, "uT": was_a}

        def feed_forward(l, b, half):
            s = l % 2
            xf = shifted(xfT[b], b, half, [], fst["xfT"][b])
            yield
            c0 = half * GROUP * P
            i, ps, marks = take()
            for k in range(GROUP):
                tok = run("tensor", lambda e, ps=ps, k=k: e.transpose(
                    ps[:, P * k:P * (k + 1)], xfT[b][:, c0 + P * k:c0 + P * (k + 1)], ident), marks + [xf])
            fst["xfT"][b] = [tok]
            nd = norm_tiles(ps.rearrange("p (t d) -> p t d", d=P), xf_n, GROUP, [tok] + fst["xf_n"])
            give(i, nd)
            yield
            i, ps, marks = take()
            for k in range(GROUP):
                tok = run("tensor", lambda e, ps=ps, k=k: e.transpose(ps[:, P * k:P * (k + 1)], xf_n[:, k, :], ident), marks + [nd])
            gel_free = [tok]
            xt = run("vector", lambda e, ps=ps: e.tensor_scalar(xf_T[:, :], ps[:, 0:BANK], vecs[s][:, 0:1], vecs[s][:, 1:2],
                                                                ALU.mult, ALU.add), [tok, W[l]] + fst["xf_T"])
            give(i, xt)
            yield
            for c, n in enumerate(ff_rows):
                i, ps, marks = take()
                for m in range(2):
                    at = m * ff + P * c
                    tok = run("tensor", lambda e, ps=ps, m=m, at=at, n=n: e.matmul(
                        ps[0:n, BANK * m:BANK * (m + 1)], w_1[s][:, at:at + n], xf_T[:, :], start=True, stop=True),
                        marks + [xt, W[l]])
                nf = len(ff_rows)
                ge = run("scalar", lambda e, ps=ps, n=n, c=c: e.activation(
                    gel[0:n, :], ps[0:n, BANK:PAIR], ACT.Gelu, bias=vecs[s][0:n, 2 + nf + c:3 + nf + c]), [tok, W[l]] + gel_free)
                u = run("vector", lambda e, ps=ps, n=n, c=c: e.scalar_tensor_tensor(
                    out=uT[0:n, c, :], in0=ps[0:n, 0:BANK], scalar=vecs[s][0:n, 2 + c:3 + c], in1=gel[0:n, :],
                    op0=ALU.add, op1=ALU.mult), [ge] + fst["uT"])
                gel_free = fst["xf_n"] = [u]
                give(i, u)
            fst["xf_T"] = [tok]
            yield
            i, ps, marks = take()
            for k in range(GROUP):
                for c, n in enumerate(ff_rows):
                    tok = run("tensor", lambda e, ps=ps, k=k, c=c, n=n: e.matmul(
                        ps[:, P * k:P * (k + 1)], uT[0:n, c, P * k:P * (k + 1)], w_2[s][0:n, c, :], start=c == 0,
                        stop=c == len(ff_rows) - 1), marks + [u])
            fst["uT"] = [tok]
            t0 = b * tiles + half * GROUP
            xg = X[:, t0:t0 + GROUP, :]
            add = run("vector", lambda e, ps=ps: e.tensor_tensor(xg, ps[:, 0:BANK].rearrange("p (t d) -> p t d", d=P), xg, ALU.add),
                      [tok])
            give(i, add)
            add = run("vector", lambda e: e.tensor_tensor(xg, xg, b2_all[s][:, :].unsqueeze(1).to_broadcast([P, GROUP, P]), ALU.add))
            for k in range(GROUP):
                x_ready[t0 + k] = add
            layer_end[l] = [tok, add]

        STAGES = ["project", "rotate", "add", "turn", "score", "exp", "weigh", "spread", "gather", "output"]
        AGE = dict(project=0, rotate=1, add=2, turn=2, score=3, exp=4, weigh=4, spread=5, gather=6, output=7)
        ORDER = ["exp", "spread", "add", "output", "gather", "weigh", "score", "feed_forward", "turn", "rotate", "project"]
        groups = tiles // GROUP
        xs_free = [was_a] * batches
        load_layer(0)
        load_layer(1)
        started = {}
        ff_jobs, ff_done = [], set()

        def feed_forward_stage():
            for job, name in list(ff_jobs):
                if next(job, "end") == "end":
                    ff_jobs.remove((job, name))
                    ff_done.add(name)
                    if name[1:] == (batches - 1, groups - 1) and name[0] + 2 < layers:
                        load_layer(name[0] + 2)

        def step(now):
            for stage in ORDER:
                if stage == "feed_forward":
                    feed_forward_stage()
                elif now - AGE[stage] in started:
                    job, (l, b, t) = started[now - AGE[stage]]
                    next(job, None)
                    if stage == "output" and t % GROUP == GROUP - 1:
                        ff_jobs.append((feed_forward(l, b, t // GROUP), (l, b, t // GROUP)))

        now = 0
        for l in range(layers):
            ready = load_qkv(l)
            for b in range(batches):
                for t in range(tiles):
                    if t % GROUP == 0:
                        while l and (l - 1, b, t // GROUP) not in ff_done:
                            step(now)
                            now += 1
                        xs_ready = shifted(xsT[b], b, t // GROUP, [], xs_free[b] + used["v"])
                    if (b, t) == (0, AGE["score"]):
                        ready["v"] = load("w_v", w_qkv[:, 2 * INNER:3 * INNER], ins["Wqkv"][l, :, 2 * INNER:3 * INNER], used["v"])
                    started[now] = attention_tile(l, b, t, ready, xs_ready), (l, b, t)
                    step(now)
                    now += 1
                    if (b, t) == (0, 0):
                        load_tables(l, ready)
        while len(ff_done) < layers * batches * groups:
            step(now)
            now += 1

        stores = []
        YA = qk_sq.rearrange("p m (t d) -> p (m t) d", d=P)
        ya_loaded = load("ya_back", YA, scratch.rearrange("b (t p) d -> p (b t) d", p=P), was_a + st["sq"])
        for t in range(all_tiles):
            fin = run("vector", lambda e, t=t: e.tensor_tensor(YA[:, t, :], X[:, t, :], YA[:, t, :], ALU.add), [ya_loaded, x_ready[t]])
        stores.append(load("out", out.rearrange("b (t p) d -> p (b t) d", p=P), YA, [fin]))
        prog.wait("sync", stores + was_a + [proj[k] for k in proj])
        with nc.Block() as block:
            prog.emit(block)


NAMES = {"L0_attn_Wq": "Wq", "L0_attn_Wk": "Wk", "L0_attn_Wv": "Wv", "L0_attn_W_O": "W_O", "L0_ffn_Wqkv": "Wqkv",
         "L0_ffn_q_scale": "q_scale", "L0_ffn_k_scale": "k_scale", "L0_ffn_Wo": "Wo", "L0_ffn_ln_g": "ln_g",
         "L0_ffn_ln_b": "ln_b", "L0_ffn_W1": "W1", "L0_ffn_b1": "b1", "L0_ffn_W2": "W2", "L0_ffn_b2": "b2",
         "L0_attn_x": "x"}


def kernel(**inputs):
    import concourse.bacc as bacc
    from concourse.bass_utils import run_bass_kernel_spmd

    nc = bacc.Bacc("TRN2", target_bir_lowering=False, num_devices=1)
    arrays = {short: np.ascontiguousarray(inputs[name]) for name, short in NAMES.items()}
    shape = arrays["x"].shape
    arrays["consts"] = mask_constants()
    arrays["tab_c"], arrays["tab_s"] = rotary_constants(shape[1])
    ins = {n: nc.dram_tensor(n, a.shape, mybir.dt.from_np(a.dtype), kind="ExternalInput").ap() for n, a in arrays.items()}
    out = nc.dram_tensor("out", shape, F32, kind="ExternalOutput").ap()
    scratch = nc.dram_tensor("scratch", shape, F32, kind="Internal").ap()
    parts_dram = nc.dram_tensor("parts_dram", [shape[0], 2, 3, P, shape[1]], BF16, kind="Internal").ap()
    build(nc, ins, out, scratch, parts_dram)
    result = run_bass_kernel_spmd(nc, [arrays], core_ids=[0])
    return result.results[0]["out"]
```

```python
from contextlib import ExitStack

import numpy as np

import concourse.bass as bass
from concourse import mybir

F32 = mybir.dt.float32
BF16 = mybir.dt.bfloat16
I32 = mybir.dt.int32
ALU = mybir.AluOpType
ACT = mybir.ActivationFunctionType
AX_X = mybir.AxisListType.X

P = 128
BANK = 512
PAIR = 2 * BANK
EPS = 1e-5
NORM_FLOOR = 1e-12
MASKED = -1e30
RSQRT_MAGIC = float(0x5F3759DF)

A_HEADS = 16
A_DIM = 8
A_SLOT = 32
A_PER_GROUP = P // A_SLOT
A_GROUPS = A_HEADS // A_PER_GROUP

HEADS = 16
HEAD_DIM = 64
HALF = HEAD_DIM // 2
WINDOW = 32
SIM_SCALE = 8.0
INNER = HEADS * HEAD_DIM
CHUNKS = INNER // P
WPT = P // WINDOW
GROUP = 4


def rotary_constants(n):
    f = np.float32
    half = np.arange(0, HEAD_DIM, 2, dtype=f)
    inv_freq = f(1.0) / np.power(f(10000.0), half / f(HEAD_DIM)).astype(f)
    t = np.arange(n, dtype=f)
    freqs = (t[:, None] * inv_freq[None, :]).astype(f)
    base = (half + f(0.4 * HEAD_DIM)) / f(1.4 * HEAD_DIM)
    power = (t - f(n // 2)) / f(WINDOW // 2)
    scale = np.power(base[None, :], power[:, None]).astype(f)
    cos, sin = np.cos(freqs), np.sin(freqs)
    tab_c = np.zeros((n, 2, HEAD_DIM), f)
    tab_s = np.zeros((n, 2, HEAD_DIM), f)
    for m, s in enumerate((scale, f(1.0) / scale)):
        tab_c[:, m, :HALF] = tab_c[:, m, HALF:] = cos * s
        tab_s[:, m, :HALF] = -sin * s
        tab_s[:, m, HALF:] = sin * s
    return tab_c, tab_s


def mask_constants():
    i = np.arange(P)
    ident = np.eye(P, dtype=np.float32)
    rows = np.where(i[None, :] <= i[:, None], 0.0, MASKED).astype(np.float32)
    r = (i % WINDOW)[:, None]
    k = np.arange(2 * WINDOW)[None, :]
    win = np.where((k >= r) & (k <= r + WINDOW), 0.0, MASKED).astype(np.float32)
    win0 = win.copy()
    win0[:WINDOW, :WINDOW] = MASKED
    own = (np.arange(A_HEADS * A_DIM)[None, :] // A_DIM == i[:, None] // A_DIM).astype(np.float32)
    return np.concatenate([ident, rows, rows.T, win, win0, own], axis=1)


class Program:

    def __init__(self, nc, ctx):
        self.nc, self.ctx = nc, ctx
        self.queues = {e: [] for e in ("tensor", "vector", "scalar", "gpsimd", "sync")}
        self.done = {e: ctx.enter_context(nc.semaphore(f"{e}_done")) for e in ("tensor", "vector", "scalar", "gpsimd")}
        self.count = {e: 0 for e in self.done}
        self.seen = {e: {} for e in self.queues}
        self.dma = {}

    def wait(self, engine, marks):
        for key, sem, value in marks:
            if self.seen[engine].get(key, 0) < value:
                self.seen[engine][key] = value
                self.queues[engine].append(lambda e, sem=sem, value=value: e.wait_ge(sem, value))

    def run(self, engine, instruction, after=(), mark=True):
        self.wait(engine, after)
        if engine != "tensor" and self.count[engine]:
            self.wait(engine, [(engine, self.done[engine], self.count[engine])])
        if not mark:
            self.queues[engine].append(instruction)
            return None
        self.count[engine] += 1
        sem = self.done[engine]
        self.queues[engine].append(lambda e: instruction(e).then_inc(sem, 1))
        return (engine, sem, self.count[engine])

    def load(self, stream, out, in_, after=(), engine="sync"):
        if stream not in self.dma:
            self.dma[stream] = [self.ctx.enter_context(self.nc.semaphore(f"dma_{stream}")), 0]
        entry = self.dma[stream]
        entry[1] += 16
        sem = entry[0]
        self.wait(engine, after)
        self.queues[engine].append(lambda e: e.dma_start(out, in_).then_inc(sem, 16))
        return (f"dma_{stream}", sem, entry[1])

    def emit(self, block):
        for name in self.queues:
            def body(engine, queue=self.queues[name]):
                for instruction in queue:
                    instruction(engine)
            {"tensor": block.tensor, "vector": block.vector, "scalar": block.scalar,
             "gpsimd": block.gpsimd, "sync": block.sync}[name](body)


def build(nc, ins, out, scratch, parts_dram):
    x, consts, tab_c, tab_s = ins["x"], ins["consts"], ins["tab_c"], ins["tab_s"]
    batches, seq, dim = x.shape
    layers = ins["Wqkv"].shape[0]
    tiles = seq // P
    all_tiles = batches * tiles
    ff = ins["W2"].shape[1]
    ff_rows = [min(P, ff - P * c) for c in range((ff + P - 1) // P)]
    assert dim == P and ins["Wqkv"].shape[2] == 3 * INNER

    with ExitStack() as ctx:
        prog = Program(nc, ctx)
        run, load = prog.run, prog.load

        def sb(name, shape, dt=F32):
            return ctx.enter_context(nc.sbuf_tensor(name, shape, dt))

        banks = ctx.enter_context(nc.psum_tensor("banks", [P, 4, PAIR], F32))
        free_pairs = [(i, []) for i in range(4)]

        def take():
            i, marks = free_pairs.pop(0)
            return i, banks[:, i, :], marks

        def give(i, *marks):
            free_pairs.append((i, list(marks)))

        ARENA = 37 * PAIR + 8
        arena = sb("arena", [P, ARENA])
        used_words = {"A": 0, "stack": 0}

        def carve(owner, words):
            at = used_words[owner]
            used_words[owner] = at + words
            assert used_words[owner] <= ARENA
            return arena[:, at:at + words]

        ident = sb("ident", [P, P])[:, :]
        cst_b = sb("cst_b", [P, 3 * P + 4 * WINDOW], BF16)
        ident_b = cst_b[:, 0:P]
        mask_rows, mask_cols = cst_b[:, P:2 * P], cst_b[:, 2 * P:3 * P]
        win_b = sb("win_b", [P, 2, 8, 2 * WINDOW], BF16)
        base_c, base_s = sb("base_c", [P, tiles, 2, HEAD_DIM]), sb("base_s", [P, tiles, 2, HEAD_DIM])
        X = sb("X", [P, all_tiles, P])
        x_loaded = [load(f"x{b}", X[:, b * tiles:(b + 1) * tiles, :], x[b].rearrange("(t p) d -> p t d", p=P))
                    for b in range(batches)]
        ident_loaded = load("const", ident, consts[:, 0:P])
        MASKS = 3 * P + 4 * WINDOW
        PARTS = 3
        ROWS = A_DIM * PARTS * PARTS
        RING = 3 * A_PER_GROUP
        last_group = batches * A_GROUPS - 1
        QS, KS = {}, {}
        for n_g in (last_group - 2, last_group - 1, last_group):
            for j in range(A_PER_GROUP):
                slot = (n_g * A_PER_GROUP + j) % RING
                QS[slot], KS[slot] = (carve("A", seq // 2).bitcast(BF16) for _ in range(2))
        cst = carve("A", MASKS + A_HEADS * A_DIM)
        cst_loaded = load("masks", cst, consts)
        own_head = cst[:, MASKS:].rearrange("p (h d) -> p h d", d=A_DIM)

        RS = 2 * HEADS
        rs_h, rs_t, rs_g = sb("rs_h", [P, RS], I32), sb("rs_t", [P, RS]), sb("rs_g", [P, RS])

        def rsqrt(y, v, n, after=(), steps_on="vector"):
            h, t = rs_h[:, 0:n], rs_t[:, 0:n]
            run("vector", lambda e: e.tensor_scalar(h, v.bitcast(I32), 1, None, ALU.logical_shift_right), after)
            last = run("vector", lambda e: e.tensor_scalar(y.bitcast(I32), h, -1.0, RSQRT_MAGIC, ALU.mult, ALU.add), after)
            if steps_on == "gpsimd":
                t = rs_g[:, 0:n]
                for _ in range(3):
                    run("gpsimd", lambda e: e.tensor_tensor(t, y, y, ALU.mult), [last])
                    run("gpsimd", lambda e: e.tensor_tensor(t, t, v, ALU.mult))
                    run("gpsimd", lambda e: e.tensor_scalar(t, t, -0.5, 1.5, ALU.mult, ALU.add))
                    last = run("gpsimd", lambda e: e.tensor_tensor(y, y, t, ALU.mult))
                return last
            for _ in range(3):
                run("vector", lambda e: e.tensor_tensor(t, y, y, ALU.mult))
                run("vector", lambda e: e.scalar_tensor_tensor(out=t, in0=t, scalar=-0.5, in1=v, op0=ALU.mult, op1=ALU.mult))
                last = run("vector", lambda e: e.scalar_tensor_tensor(out=y, in0=t, scalar=1.5, in1=y, op0=ALU.add, op1=ALU.mult))
            return last

        stats = sb("stats", [P, 6])
        mean_var = sb("mean_var", [P, all_tiles, 2])
        ln_v, ln_r = sb("ln_v", [P, all_tiles]), sb("ln_r", [P, all_tiles])

        def norm_tiles(src, dst, n, after):
            for i in range(n):
                run("vector", lambda e, i=i: e.bn_stats(stats[:, :], src[:, i, :]), after if i == 0 else ())
                run("vector", lambda e, i=i: e.bn_aggr(mean_var[:, i, :], stats[:, :]))
            run("vector", lambda e: e.tensor_scalar(ln_v[:, 0:n], mean_var[:, 0:n, 1], EPS, None, ALU.add))
            rsqrt(ln_r[:, 0:n], ln_v[:, 0:n], n)
            for i in range(n):
                last = run("vector", lambda e, i=i: e.tensor_scalar(
                    dst[:, i, :], src[:, i, :], mean_var[:, i, 0:1], ln_r[:, i:i + 1], ALU.subtract, ALU.mult))
            return last

        x_ready = []

        w_qkv = sb("w_qkv", [P, 3 * INNER])
        w_o = [sb(f"w_o{s}", [P, CHUNKS, P]) for s in range(2)]
        w_1 = [sb(f"w_1{s}", [P, 2 * ff]) for s in range(2)]
        w_2 = [sb(f"w_2{s}", [P, len(ff_rows), P]) for s in range(2)]
        vecs = [sb(f"vecs{s}", [P, 2 + 2 * len(ff_rows)]) for s in range(2)]
        b2_all = [sb(f"b2_all{s}", [P, P]) for s in range(2)]
        qk_gain = sb("qk_gain", [P, 2, HEAD_DIM])
        tab_cl, tab_sl = sb("tab_cl", [P, tiles, 2, HEAD_DIM]), sb("tab_sl", [P, tiles, 2, HEAD_DIM])

        W = {}
        layer_end = {}
        used = {"qk": [], "v": [], "tabs": []}

        def load_layer(l):
            s = l % 2
            free = layer_end.get(l - 2, [])
            load(f"w{s}", w_o[s][:, :, :], ins["Wo"][l].rearrange("(c p) d -> p c d", p=P), free)
            load(f"w{s}", w_1[s][:, :], ins["W1"][l])
            for c, n in enumerate(ff_rows):
                load(f"w{s}", w_2[s][0:n, c, :], ins["W2"][l, P * c:P * c + n, :])
                for m in range(2):
                    at = m * ff + P * c
                    load(f"w{s}", vecs[s][0:n, 2 + m * len(ff_rows) + c:3 + m * len(ff_rows) + c],
                         ins["b1"][l, at:at + n].rearrange("(p a) -> p a", a=1))
            load(f"w{s}", vecs[s][:, 0:1], ins["ln_g"][l].rearrange("(p a) -> p a", a=1))
            load(f"w{s}", vecs[s][:, 1:2], ins["ln_b"][l].rearrange("(p a) -> p a", a=1))
            W[l] = load(f"w{s}", b2_all[s][:, :], ins["b2"][l:l + 1, :].to_broadcast([P, P]))

        def load_qkv(l):
            ready = {"qk": load("w_qk", w_qkv[:, 0:2 * INNER], ins["Wqkv"][l, :, 0:2 * INNER], used["qk"])}
            return ready

        def load_tables(l, ready):
            load("gain", qk_gain[:, 0, :], ins["q_scale"][l:l + 1, :].to_broadcast([P, HEAD_DIM]), used["tabs"])
            gain = load("gain", qk_gain[:, 1, :], ins["k_scale"][l:l + 1, :].to_broadcast([P, HEAD_DIM]))
            g = qk_gain[:, :, :].unsqueeze(1).to_broadcast([P, tiles, 2, HEAD_DIM])
            run("gpsimd", lambda e: e.tensor_tensor(tab_cl[:, :, :, :], base_c[:, :, :, :], g, ALU.mult), [gain, tabs_loaded] + used["tabs"])
            for d, s in ((0, HALF), (HALF, 0)):
                gs = qk_gain[:, :, s:s + HALF].unsqueeze(1).to_broadcast([P, tiles, 2, HALF])
                tabs = run("gpsimd", lambda e, d=d, gs=gs: e.tensor_tensor(
                    tab_sl[:, :, :, d:d + HALF], base_s[:, :, :, d:d + HALF], gs, ALU.mult))
            ready["tabs"] = tabs

        w_diag = [carve("A", P) for m in range(2)]
        w_pad = carve("A", A_HEADS * A_SLOT).rearrange("p (h d) -> p h d", d=A_SLOT)
        xnT = carve("A", seq)
        parts = carve("A", PARTS * seq // 2).bitcast(BF16).rearrange("p (s n) -> p s n", s=PARTS)
        rest = carve("A", seq)
        m_neg = [carve("A", tiles * A_PER_GROUP).rearrange("p (t j) -> p t j", j=A_PER_GROUP) for _ in range(2)]
        m_parts = [carve("A", PARTS * seq // 2).bitcast(BF16).rearrange("p (s n) -> p s n", s=PARTS) for _ in range(2)]
        m_rest = carve("A", seq)
        ones_b = carve("A", seq // 2).bitcast(BF16)
        w_rows = [carve("A", A_DIM) for _ in range(3)]
        w_out_a = carve("A", P)
        VA = carve("A", tiles * A_HEADS * A_SLOT).rearrange("p (t h d) -> p t h d", h=A_HEADS, d=A_SLOT)
        pt_ring = [carve("A", seq) for _ in range(4)]
        accT = carve("A", seq)
        a_sum = carve("A", tiles * A_PER_GROUP).rearrange("p (t j) -> p t j", j=A_PER_GROUP)
        xa = carve("A", seq).rearrange("p (t d) -> p t d", d=P)
        ya = carve("A", seq).rearrange("p (t d) -> p t d", d=P)
        cat = carve("A", all_tiles * P).rearrange("p (t d) -> p t d", d=P)

        for m, name in enumerate(("Wq", "Wk", "Wv")):
            w_in = load("w_a", w_rows[m], ins[name].rearrange("h d e -> (h d) e"))
        zeroed = run("gpsimd", lambda e: e.memset(w_pad, 0.0))
        for m in range(3):
            dst = w_pad[:, :, 0:A_DIM] if m == 2 else w_diag[m].rearrange("p (h d) -> p h d", d=A_DIM)
            w_loaded = run("gpsimd", lambda e, m=m, dst=dst: e.tensor_tensor(
                dst, w_rows[m].unsqueeze(1).to_broadcast([P, A_HEADS, A_DIM]), own_head, ALU.mult), [w_in, cst_loaded])
        ones_set = run("gpsimd", lambda e: e.memset(ones_b[0:PARTS, :], 1.0))
        wo_a_loaded = load("w_out_a", w_out_a, ins["W_O"])
        for s in range(RING):
            ones_stored = load("ones", KS[s][ROWS:ROWS + PARTS, :], ones_b[0:PARTS, :], [ones_set])

        def split(src, dst, spare, after, free):
            hi = run("scalar", lambda e: e.copy(dst[:, 0, :], src), after + free)
            v1 = run("vector", lambda e: e.tensor_tensor(spare, src, dst[:, 0, :], ALU.subtract), [hi])
            mid = run("scalar", lambda e: e.copy(dst[:, 1, :], spare), [v1])
            lo = run("vector", lambda e: e.tensor_tensor(dst[:, 2, :], spare, dst[:, 1, :], ALU.subtract), [mid])
            return v1, lo

        pt_free = [[], [], [], []]
        a_state = {"turn": 0, "xnT": [], "acc": [], "VA": [], "parts": []}
        stack_free = [[] for _ in range(RING)]
        stack_ready, row_ready, proj = {}, {}, {}
        maxima_end = []

        def project(b):
            i, ps, marks = take()
            for t in range(tiles):
                tok = run("tensor", lambda e, ps=ps, t=t: e.transpose(ps[:, P * t:P * (t + 1)], X[:, b * tiles + t, :], ident),
                          marks + [ident_loaded, x_ready[b * tiles + t]])
            xnT_ready = run("scalar", lambda e, ps=ps: e.copy(xnT, ps), [tok] + a_state["xnT"])
            give(i, xnT_ready)
            for m in range(2):
                i, ps, marks = take()
                for c in range(seq // BANK):
                    tok = run("tensor", lambda e, ps=ps, m=m, c=c: e.matmul(
                        ps[:, BANK * c:BANK * (c + 1)], w_diag[m], xnT[:, BANK * c:BANK * (c + 1)], start=True, stop=True),
                        marks + [xnT_ready, w_loaded])
                v1, lo = split(ps, parts, rest, [tok], a_state["parts"])
                give(i, v1)
                proj[b, m] = load(f"parts{m}", parts_dram[b, m], parts, [lo])
                a_state["parts"] = [proj[b, m]]
            yield

        def project_v(b):
            for t in range(tiles):
                i, ps, marks = take()
                tok = run("tensor", lambda e, ps=ps, t=t: e.matmul(
                    ps[:, 0:BANK], xnT[:, P * t:P * (t + 1)], w_pad.rearrange("p h d -> p (h d)"), start=True, stop=True), marks)
                va = run("scalar", lambda e, ps=ps, t=t: e.copy(VA[:, t, :, :].rearrange("p h d -> p (h d)"), ps[:, 0:BANK]),
                         [tok] + a_state["VA"])
                give(i, va)
            a_state["xnT"] = [tok]
            a_state["VA_ready"] = run("gpsimd", lambda e: e.memset(VA[:, :, :, A_DIM:A_DIM + 1], 1.0), [va])

        def load_stacks(b, g):
            for j in range(A_PER_GROUP):
                h = g * A_PER_GROUP + j
                slot = ((b * A_GROUPS + g) * A_PER_GROUP + j) % RING
                q, k = (parts_dram[b, m, A_DIM * h:A_DIM * (h + 1), :, :] for m in range(2))
                wait = stack_free[slot] + [proj[b, 0], proj[b, 1]]
                for s in range(PARTS):
                    rows = slice(ROWS // PARTS * s, ROWS // PARTS * (s + 1))
                    load(f"stack{slot}", QS[slot][rows, :], q[:, s:s + 1, :].to_broadcast([A_DIM, PARTS, seq]), wait)
                done = load(f"stack{slot}", KS[slot][0:ROWS, :],
                            k.rearrange("d r n -> (d r) n").unsqueeze(0).to_broadcast([PARTS, ROWS // PARTS, seq]), wait)
                stack_ready[b, g, j] = done

        def row_maxima(b, g):
            n_g = b * A_GROUPS + g
            mn, mp = m_neg[n_g % 2], m_parts[n_g % 2]
            slots = [(n_g * A_PER_GROUP + j) % RING for j in range(A_PER_GROUP)]
            for qt in reversed(range(tiles)):
                n = P * (qt + 1)
                for j, slot in enumerate(slots):
                    i, ps, marks = take()
                    for c in range((n + BANK - 1) // BANK):
                        e1 = min(n, BANK * (c + 1))
                        run("tensor", lambda e, ps=ps, slot=slot, qt=qt, c=c, e1=e1: e.matmul(
                            ps[:, BANK * c:e1], QS[slot][0:ROWS, P * qt:P * (qt + 1)], KS[slot][0:ROWS, BANK * c:e1],
                            start=True, stop=True), marks + [stack_ready[b, g, j]], mark=False)
                    tok = run("tensor", lambda e, ps=ps, n=n: e.matmul(
                        ps[:, n - P:n], ident_b, mask_rows, start=False, stop=True, skip_group_check=True), [c_ready])
                    mx = run("vector", lambda e, ps=ps, n=n, qt=qt, j=j: e.tensor_reduce(
                        mn[:, qt, j:j + 1], ps[:, 0:n], AX_X, ALU.max, negate=True), [tok])
                    give(i, mx)
                    yield
            i, ps, marks = take()
            for t in range(tiles):
                tok = run("tensor", lambda e, ps=ps, t=t: e.transpose(ps[0:A_PER_GROUP, P * t:P * (t + 1)], mn[:, t, :], ident),
                          marks + [mx])
            rows4 = slice(0, A_PER_GROUP)
            v1, lo = split(ps[rows4], mp[rows4], m_rest[rows4], [tok], a_state.get(("mp", n_g % 2), []))
            give(i, v1)
            for j, slot in enumerate(slots):
                for s in range(PARTS):
                    row_ready[b, g, j] = load(f"rows{slot}", QS[slot][ROWS + s:ROWS + s + 1, :], mp[j:j + 1, s, :], [lo])
            maxima_end[:] = [lo, v1, tok] + [row_ready[b, g, j] for j in range(A_PER_GROUP)]
            a_state["mp", n_g % 2] = [row_ready[b, g, j] for j in range(A_PER_GROUP)]
            yield

        def weigh(b, g):
            acc_i, acc, acc_marks = take()
            for kt in range(tiles):
                q0 = P * kt
                for j in range(A_PER_GROUP):
                    slot = ((b * A_GROUPS + g) * A_PER_GROUP + j) % RING
                    h = g * A_PER_GROUP + j
                    i, ps, marks = take()
                    spans = [(max(q0, BANK * c), BANK * (c + 1)) for c in range(seq // BANK) if q0 < BANK * (c + 1)]
                    for s0, s1 in spans:
                        tok = run("tensor", lambda e, ps=ps, slot=slot, kt=kt, s0=s0, s1=s1: e.matmul(
                            ps[:, s0:s1], KS[slot][0:ROWS + PARTS, P * kt:P * (kt + 1)], QS[slot][0:ROWS + PARTS, s0:s1],
                            start=True, stop=True), marks + [row_ready[b, g, j], ones_stored])
                        if s0 == q0:
                            tok = run("tensor", lambda e, ps=ps, q0=q0: e.matmul(
                                ps[:, q0:q0 + P], ident_b, mask_cols, start=False, stop=True, skip_group_check=True))
                    if kt == tiles - 1:
                        stack_free[slot] = [tok]
                    turn = a_state["turn"]
                    buf, was = pt_ring[turn], pt_free[turn]
                    ex = run("scalar", lambda e, ps=ps, buf=buf, q0=q0: e.activation(
                        buf[:, q0:seq], ps[:, q0:seq], ACT.Exp, scale=float(A_DIM) ** -0.5), [tok] + was)
                    give(i, ex)
                    late.append((j, kt, h, buf, spans, ex, turn))
                    a_state["turn"] = (turn + 1) % 4
                    if len(late) > 2:
                        gather(acc, acc_marks, *late.pop(0))
                    yield
            while late:
                gather(acc, acc_marks, *late.pop(0))
            tok = a_state["gathered"]
            at = run("scalar", lambda e: e.copy(accT, acc), [tok] + a_state["acc"])
            give(acc_i, at)
            i, ps, marks = take()
            for t in range(tiles):
                tok = run("tensor", lambda e, ps=ps, t=t: e.transpose(ps[:, P * t:P * (t + 1)], accT[:, P * t:P * (t + 1)], ident),
                          marks + [at])
            a_state["acc"] = [tok]
            psv = ps.rearrange("p (t j c) -> p t j c", j=A_PER_GROUP, c=A_SLOT)
            run("vector", lambda e: e.reciprocal(a_sum, psv[:, :, :, A_DIM]), [tok])
            last = run("vector", lambda e: e.tensor_tensor(
                cat[:, b * tiles:(b + 1) * tiles, :].rearrange("p t (g j d) -> p t g j d", j=A_PER_GROUP, d=A_DIM)[:, :, g],
                psv[:, :, :, 0:A_DIM], a_sum.unsqueeze(3).to_broadcast([P, tiles, A_PER_GROUP, A_DIM]), ALU.mult))
            give(i, last)
            a_state["VA"] = [tok]
            a_state["cat"] = last
            yield

        late = []

        def gather(acc, acc_marks, j, kt, h, buf, spans, ex, turn):
            for s0, s1 in spans:
                tok = run("tensor", lambda e, s0=s0, s1=s1: e.matmul(
                    acc[A_SLOT * j:A_SLOT * (j + 1), s0:s1], VA[:, kt, h, :], buf[:, s0:s1],
                    start=kt == 0, stop=True, skip_group_check=True), acc_marks + [ex, a_state["VA_ready"]])
            pt_free[turn] = [tok]
            a_state["gathered"] = tok

        def output_a(b):
            was = a_state.get("ya", [])
            xa_loaded = load("xa", xa, x[b].rearrange("(e t) d -> e t d", t=tiles), was)
            i, ps, marks = take()
            for t in range(tiles):
                tok = run("tensor", lambda e, ps=ps, t=t: e.matmul(
                    ps[:, P * t:P * (t + 1)], cat[:, b * tiles + t, :], w_out_a, start=True, stop=True),
                    marks + [a_state["cat"], wo_a_loaded])
            y_ready = run("vector", lambda e, ps=ps: e.tensor_tensor(
                ya.rearrange("p t d -> p (t d)"), ps, xa.rearrange("p t d -> p (t d)"), ALU.add), [tok, xa_loaded] + was)
            give(i, y_ready)
            a_state["ya"] = [load("ya", scratch[b].rearrange("(e t) d -> e t d", t=tiles), ya, [y_ready]), y_ready]
            a_state["end"] = [tok, y_ready, a_state["ya"][0]]

        order = [(b, g) for b in range(batches) for g in range(A_GROUPS)]
        LAG = 12

        def maxima_stream():
            for n_g, (b, g) in enumerate(order):
                for _ in row_maxima(b, g):
                    yield
                if (g, b + 1 < batches) == (A_GROUPS - 3, True):
                    for _ in project(b + 1):
                        pass

        def weigh_stream():
            for n_g, (b, g) in enumerate(order):
                for _ in weigh(b, g):
                    yield
                a_state["weighed"] = n_g
                if g == A_GROUPS - 1:
                    output_a(b)
                    if b + 1 < batches:
                        project_v(b + 1)
                if n_g + 3 < len(order):
                    load_stacks(*order[n_g + 3])

        for b in range(batches):
            xb = X[:, b * tiles:(b + 1) * tiles, :]
            x_ready += [norm_tiles(xb, xb, tiles, [x_loaded[b]])] * tiles
            if b == 0:
                c_ready = run("vector", lambda e: e.tensor_copy(cst_b[:, :], cst[:, 0:MASKS]), [cst_loaded])
                for m in range(2):
                    at = 3 * P + 2 * WINDOW * m
                    c_ready = run("vector", lambda e, m=m, at=at: e.tensor_copy(
                        win_b[:, m, :, :], cst_b[:, at:at + 2 * WINDOW].unsqueeze(1).to_broadcast([P, 8, 2 * WINDOW])))
                for _ in project(0):
                    pass
        for n_g in range(3):
            load_stacks(*order[n_g])
        project_v(0)
        for tab, src in ((base_c, tab_c), (base_s, tab_s)):
            tabs_loaded = load("tabs", tab[:, :, :, :], src.rearrange("(t p) m d -> p t m d", p=P))
        load_layer(0)
        load_layer(1)
        ready0 = load_qkv(0)
        ready0["v"] = load("w_v", w_qkv[:, 2 * INNER:3 * INNER], ins["Wqkv"][0, :, 2 * INNER:3 * INNER])
        load_tables(0, ready0)
        maxima, weighing = maxima_stream(), weigh_stream()
        for _ in range(tiles * A_PER_GROUP + 1 + LAG):
            next(maxima)
        while next(maxima, "end") != "end":
            next(weighing)
        while a_state["weighed"] < last_group - 1:
            next(weighing)
        last_b, last_g = order[-1]
        early = [maxima_end[0], w_loaded, ones_stored, proj[last_b, 0], proj[last_b, 1]] + a_state["xnT"] + maxima_end[1:]

        def stack(*shape):
            flat = carve("stack", int(np.prod(shape)))
            names = " ".join("abc"[:len(shape)])
            return flat.rearrange(f"p ({names}) -> p {names}", **{k: v for k, v in zip("abc", shape)}) if len(shape) > 1 else flat

        PTs = [stack(2 * HEADS, P).rearrange("p (s h) q -> p s h q", s=2) for _ in range(2)]
        xfT = [stack(seq + 1) for b in range(batches)]
        PB, QT = stack(HEADS, 2 * WINDOW), stack(CHUNKS, P)
        xsT = [stack(seq + 1) for b in range(batches)]
        qk_raw = [stack(2, INNER) for _ in range(2)]
        qk_sq, qk_sw, qk_rot = stack(2, INNER), stack(2, INNER), stack(2, INNER)
        PBT = stack(2 * INNER // 2)
        KT = [stack(CHUNKS, WINDOW + P) for s in range(2)]
        V = [stack(INNER) for s in range(3)]
        Vp = [stack(INNER) for s in range(3)]
        ss, rn = sb("ss", [P, 2 * HEADS]), sb("rn", [P, 2 * HEADS])
        mx_t, sm_t, rs_o = sb("mx_t", [P, HEADS]), sb("sm_t", [P, HEADS]), sb("rs_o", [P, HEADS])
        OT = stack(CHUNKS, P)
        xf_n, xf_T = stack(GROUP, P), stack(GROUP * P)
        gel, uT = xf_n.rearrange("p t d -> p (t d)"), stack(len(ff_rows), GROUP * P)

        group_slots = [[(n_g * A_PER_GROUP + j) % RING for j in range(A_PER_GROUP)] for n_g in range(last_group - 2, last_group + 1)]
        for PT, slots in zip(PTs, group_slots):
            pt_zero = run("gpsimd", lambda e, PT=PT: e.memset(PT, 0.0), [m for slot in slots for m in stack_free[slot]])
        for b in range(batches):
            xs_zero = run("gpsimd", lambda e, b=b: e.memset(xsT[b][HEAD_DIM:P, 0:1], 0.0), early)

        def shifted(dst, b, half, after, free):
            i, ps, marks = take()
            for k in range(GROUP):
                t = b * tiles + half * GROUP + k
                tok = run("tensor", lambda e, ps=ps, k=k, t=t: e.transpose(ps[:, P * k:P * (k + 1)], X[:, t, :], ident),
                          marks + [x_ready[t]] + after)
            c0 = half * GROUP * P
            run("scalar", lambda e: e.copy(dst[0:64, c0:c0 + GROUP * P], ps[0:64, 0:GROUP * P]), [tok, xs_zero] + free)
            done = run("scalar", lambda e: e.copy(dst[64:P, c0 + 1:c0 + 1 + GROUP * P], ps[64:P, 0:GROUP * P]))
            give(i, done)
            return done

        was_a = []
        st = {"V": [was_a] * 3, "Vp": [was_a] * 3, "KT": [was_a] * 2, "KTready": [None, None],
              "raw": [early] * len(qk_raw), "sq": early, "rn": [], "sw": was_a, "PBT": was_a, "rot0": was_a, "rot1": was_a, "PT": [was_a] * 2, "PB": was_a, "QT": was_a, "OT": was_a,
              "n": 0}

        def attention_tile(l, b, t, ready, xs_ready):
            n = st["n"]
            st["n"] += 1
            s = l % 2
            first = t == 0
            lhs = xsT[b][:, P * t:P * (t + 1)]
            raw, rot = qk_raw[n % len(qk_raw)], qk_rot
            for m in range(2):
                i, ps, marks = take()
                for c in range(2):
                    at = m * INNER + BANK * c
                    tok = run("tensor", lambda e, ps=ps, c=c, at=at: e.matmul(
                        ps[:, BANK * c:BANK * (c + 1)], lhs, w_qkv[:, at:at + BANK], start=True, stop=True),
                        marks + [ready["qk"], xs_ready])
                run("scalar", lambda e, ps=ps, m=m: e.copy(raw[:, m, :], ps), [tok] + st["raw"][n % len(qk_raw)])
                sq = run("scalar", lambda e, ps=ps, m=m: e.activation(qk_sq[:, m, :], ps, ACT.Square), st["sq"])
                give(i, sq)
            used["qk"] = [tok]
            yield
            def heads(a):
                return a.rearrange("p m (h d) -> p (m h) d", d=HEAD_DIM)

            rd = run("vector", lambda e: e.tensor_reduce(ss[:, :], heads(qk_sq), AX_X, ALU.add), [sq] + st["rn"])
            st["sq"] = [rd]
            run("vector", lambda e: e.tensor_scalar(ss[:, :], ss[:, :], NORM_FLOOR ** 2, None, ALU.max))
            rn_ready = rsqrt(rn[:, :], ss[:, :], 2 * HEADS, st["rn"], "gpsimd")
            yield
            for m in range(2):
                qn = run("vector", lambda e, m=m: e.tensor_tensor(
                    raw[:, m, :].rearrange("p (h d) -> p h d", d=HEAD_DIM), raw[:, m, :].rearrange("p (h d) -> p h d", d=HEAD_DIM),
                    rn[:, HEADS * m:HEADS * (m + 1)].unsqueeze(2).to_broadcast([P, HEADS, HEAD_DIM]), ALU.mult), [rn_ready])
                for d, o in ((0, HALF), (HALF, 0)):
                    src = raw[:, m, :].rearrange("p (h d) -> p h d", d=HEAD_DIM)[:, :, o:o + HALF]
                    dst = qk_sw[:, m, :].rearrange("p (h d) -> p h d", d=HEAD_DIM)[:, :, d:d + HALF]
                    tb = tab_sl[:, t, m, d:d + HALF].unsqueeze(1).to_broadcast([P, HEADS, HALF])
                    sw = run("gpsimd", lambda e, dst=dst, src=src, tb=tb: e.tensor_tensor(dst, src, tb, ALU.mult),
                             [qn, ready["tabs"]] + st["sw"])
                st["swm"] = st.get("swm", {})
                st["swm"][m] = sw
            for m in range(2):
                rc = run("vector", lambda e, m=m: e.tensor_tensor(
                    rot[:, m, :].rearrange("p (h d) -> p h d", d=HEAD_DIM), raw[:, m, :].rearrange("p (h d) -> p h d", d=HEAD_DIM),
                    tab_cl[:, t, m, :].unsqueeze(1).to_broadcast([P, HEADS, HEAD_DIM]), ALU.mult),
                    [ready["tabs"]] + st["rot%d" % m])
            used["tabs"] = [sw, rc]
            st["rn"] = [rn_ready, rc]
            st["raw"][n % len(qk_raw)] = [sw, rc]
            swm = dict(st["swm"])
            yield
            rotated = {m: run("vector", lambda e, m=m: e.tensor_tensor(rot[:, m, :], rot[:, m, :], qk_sw[:, m, :], ALU.add), [swm[m]])
                       for m in (1, 0)}
            st["sw"] = [rotated[0]]
            yield
            kt_buf = KT[n % 2]
            for m in (1, 0):
                i, ps, marks = take()
                for c in range(CHUNKS):
                    tok = run("tensor", lambda e, ps=ps, c=c, m=m: e.transpose(
                        ps[:, P * c:P * (c + 1)], rot[:, m, P * c:P * (c + 1)], ident), marks + [rotated[m]])
                st["rot%d" % m] = [tok]
                if m:
                    k_ready = run("scalar", lambda e, ps=ps: e.copy(
                        kt_buf[:, :, WINDOW:WINDOW + P], ps.rearrange("p (c q) -> p c q", q=P)), [tok] + st["KT"][n % 2])
                    give(i, k_ready)
                else:
                    q_ready = run("scalar", lambda e, ps=ps: e.copy(QT.rearrange("p c q -> p (c q)"), ps), [tok] + st["QT"])
                    give(i, q_ready)
            if first:
                kp = run("gpsimd", lambda e: e.memset(kt_buf[:, :, 0:WINDOW], 0.0), st["KT"][n % 2])
            else:
                before = KT[(n - 1) % 2]
                kp = run("gpsimd", lambda e: e.tensor_copy(kt_buf[:, :, 0:WINDOW], before[:, :, P:P + WINDOW]),
                         st["KT"][n % 2] + [st["KTready"][(n - 1) % 2]])
            st["KTready"][n % 2] = k_ready
            yield
            i, ps, marks = take()
            for half in range(2):
                run("tensor", lambda e, ps=ps, half=half: e.matmul(
                    ps[:, BANK * half:BANK * (half + 1)], ident_b, win_b[:, int(first), :, :].rearrange("p c k -> p (c k)"),
                    start=True, stop=True), marks + [c_ready], mark=False)
            for c in range(CHUNKS):
                for half in range(2):
                    for w in range(WPT):
                        r = slice(64 * half, 64 * half + 64)
                        col = BANK * half + 2 * WINDOW * c
                        tok = run("tensor", lambda e, ps=ps, r=r, c=c, w=w, col=col: e.matmul(
                            ps[WINDOW * w:WINDOW * (w + 1), col:col + 2 * WINDOW], QT[r, c, WINDOW * w:WINDOW * (w + 1)],
                            kt_buf[r, c, WINDOW * w:WINDOW * (w + 2)], start=False, stop=True, skip_group_check=True),
                            [q_ready, k_ready, kp], mark=c == CHUNKS - 1 and w == WPT - 1 and half == 1)
            st["QT"] = [tok]
            st["KT"][n % 2] = [tok]
            st["KT"][(n - 1) % 2] = st["KT"][(n - 1) % 2] + [kp]
            sc = ps.rearrange("p (h k) -> p h k", k=2 * WINDOW)
            run("vector", lambda e: e.tensor_reduce(mx_t[:, :], sc, AX_X, ALU.max), [tok])
            sub = run("vector", lambda e: e.tensor_tensor(PB, sc, mx_t[:, :].unsqueeze(2).to_broadcast([P, HEADS, 2 * WINDOW]),
                                                          ALU.subtract), st["PB"])
            give(i, sub)
            i, ps, marks = take()
            for c in range(2):
                at = 2 * INNER + BANK * c
                tok = run("tensor", lambda e, ps=ps, c=c, at=at: e.matmul(
                    ps[:, BANK * c:BANK * (c + 1)], lhs, w_qkv[:, at:at + BANK], start=True, stop=True), marks + [ready["v"]])
            used["v"] = [tok]
            v, vp = V[n % 3], Vp[n % 3]
            v_ready = run("scalar", lambda e, ps=ps: e.copy(v, ps), [tok] + st["V"][n % 3])
            give(i, v_ready)
            if first:
                vp_marks = [run("gpsimd", lambda e: e.memset(vp[0:WINDOW, :], 0.0), st["Vp"][n % 3])]
            else:
                prev = V[(n - 1) % 3]
                vp_marks = [load(f"vp_head{n % 3}", vp[0:WINDOW, :], prev[P - WINDOW:P, :], st["Vp"][n % 3])]
            vp_marks.append(load(f"vp_body{n % 3}", vp[WINDOW:P, :], v[0:P - WINDOW, :], [v_ready] + st["Vp"][n % 3]))
            st["V"][n % 3] = [vp_marks[-1]]
            if not first:
                st["V"][(n - 1) % 3] = st["V"][(n - 1) % 3] + [vp_marks[0]]
            yield
            ex = run("scalar", lambda e: e.activation(PB, PB, ACT.Exp, scale=SIM_SCALE), [sub])
            yield
            run("vector", lambda e: e.tensor_reduce(sm_t[:, :], PB, AX_X, ALU.add), [ex])
            run("vector", lambda e: e.reciprocal(rs_o[:, :], sm_t[:, :]))
            run("vector", lambda e: e.tensor_tensor(PB, PB, rs_o[:, :].unsqueeze(2).to_broadcast([P, HEADS, 2 * WINDOW]), ALU.mult))
            bt = run("vector", lambda e: e.transpose(PBT, PB), st["PBT"])
            st["PB"] = [bt]
            yield
            PT = PTs[n % 2]
            for w in range(WPT):
                r = slice(WINDOW * w, WINDOW * (w + 1))
                pt = run("scalar", lambda e, r=r: e.copy(
                    PT[r, :, :, r].rearrange("p s h q -> p h s q"), PBT.rearrange("p (h s q) -> p h s q", s=2, q=WINDOW)[r]),
                    [bt, pt_zero] + st["PT"][n % 2])
            st["PBT"] = [pt]
            yield
            i, ps, marks = take()
            for c in range(CHUNKS):
                for src, prior in ((v, 0), (vp, 1)):
                    for half in range(2):
                        hh = half * CHUNKS + c
                        vs = slice(HEAD_DIM * (2 * c + half), HEAD_DIM * (2 * c + half + 1))
                        tok = run("tensor", lambda e, ps=ps, c=c, src=src, prior=prior, half=half, hh=hh, vs=vs: e.matmul(
                            ps[64 * half:64 * half + 64, P * c:P * (c + 1)], src[:, vs], PT[:, 1 - prior, hh, :],
                            start=not prior, stop=bool(prior)), marks + [pt, v_ready] + vp_marks, mark=c == CHUNKS - 1)
            st["PT"][n % 2] = [tok]
            st["V"][n % 3] = st["V"][n % 3] + [tok]
            st["Vp"][n % 3] = [tok]
            ot = run("scalar", lambda e, ps=ps: e.copy(OT.rearrange("p c q -> p (c q)"), ps), [tok] + st["OT"])
            give(i, ot)
            yield
            i, ps, marks = take()
            for c in range(CHUNKS):
                tok = run("tensor", lambda e, ps=ps, c=c: e.matmul(ps[:, 0:P], OT[:, c, :], w_o[s][:, c, :], start=c == 0,
                                                                   stop=c == CHUNKS - 1), marks + [ot, W[l]])
            st["OT"] = [tok]
            x_ready[b * tiles + t] = run("vector", lambda e, ps=ps: e.tensor_tensor(
                X[:, b * tiles + t, :], ps[:, 0:P], X[:, b * tiles + t, :], ALU.add), [tok])
            give(i, x_ready[b * tiles + t])

        xf_zero = []
        fst = {"xfT": [was_a] * 2, "xf_n": was_a, "xf_T": was_a, "uT": was_a}

        def feed_forward(l, b, half):
            s = l % 2
            xf = shifted(xfT[b], b, half, [], fst["xfT"][b] + xf_zero)
            yield
            c0 = half * GROUP * P
            i, ps, marks = take()
            for k in range(GROUP):
                tok = run("tensor", lambda e, ps=ps, k=k: e.transpose(
                    ps[:, P * k:P * (k + 1)], xfT[b][:, c0 + P * k:c0 + P * (k + 1)], ident), marks + [xf])
            fst["xfT"][b] = [tok]
            nd = norm_tiles(ps.rearrange("p (t d) -> p t d", d=P), xf_n, GROUP, [tok] + fst["xf_n"])
            give(i, nd)
            yield
            i, ps, marks = take()
            for k in range(GROUP):
                tok = run("tensor", lambda e, ps=ps, k=k: e.transpose(ps[:, P * k:P * (k + 1)], xf_n[:, k, :], ident), marks + [nd])
            gel_free = [tok]
            xt = run("vector", lambda e, ps=ps: e.tensor_scalar(xf_T[:, :], ps[:, 0:BANK], vecs[s][:, 0:1], vecs[s][:, 1:2],
                                                                ALU.mult, ALU.add), [tok, W[l]] + fst["xf_T"])
            give(i, xt)
            yield
            for c, n in enumerate(ff_rows):
                i, ps, marks = take()
                for m in range(2):
                    at = m * ff + P * c
                    tok = run("tensor", lambda e, ps=ps, m=m, at=at, n=n: e.matmul(
                        ps[0:n, BANK * m:BANK * (m + 1)], w_1[s][:, at:at + n], xf_T[:, :], start=True, stop=True),
                        marks + [xt, W[l]])
                nf = len(ff_rows)
                ge = run("scalar", lambda e, ps=ps, n=n, c=c: e.activation(
                    gel[0:n, :], ps[0:n, BANK:PAIR], ACT.Gelu, bias=vecs[s][0:n, 2 + nf + c:3 + nf + c]), [tok, W[l]] + gel_free)
                u = run("vector", lambda e, ps=ps, n=n, c=c: e.scalar_tensor_tensor(
                    out=uT[0:n, c, :], in0=ps[0:n, 0:BANK], scalar=vecs[s][0:n, 2 + c:3 + c], in1=gel[0:n, :],
                    op0=ALU.add, op1=ALU.mult), [ge] + fst["uT"])
                gel_free = fst["xf_n"] = [u]
                give(i, u)
            fst["xf_T"] = [tok]
            yield
            i, ps, marks = take()
            for k in range(GROUP):
                for c, n in enumerate(ff_rows):
                    tok = run("tensor", lambda e, ps=ps, k=k, c=c, n=n: e.matmul(
                        ps[:, P * k:P * (k + 1)], uT[0:n, c, P * k:P * (k + 1)], w_2[s][0:n, c, :], start=c == 0,
                        stop=c == len(ff_rows) - 1), marks + [u])
            fst["uT"] = [tok]
            t0 = b * tiles + half * GROUP
            xg = X[:, t0:t0 + GROUP, :]
            add = run("vector", lambda e, ps=ps: e.tensor_tensor(xg, ps[:, 0:BANK].rearrange("p (t d) -> p t d", d=P), xg, ALU.add),
                      [tok])
            give(i, add)
            add = run("gpsimd", lambda e: e.tensor_tensor(xg, xg, b2_all[s][:, :].unsqueeze(1).to_broadcast([P, GROUP, P]), ALU.add), [add])
            for k in range(GROUP):
                x_ready[t0 + k] = add
            layer_end[l] = [tok, add]

        AGE = dict(project=0, norm=1, rotate=1, add=2, turn=2, score=3, exp=4, weigh=4, spread=5, gather=6, output=7)
        ORDER = ["norm", "exp", "spread", "add", "output", "gather", "weigh", "score", "feed_forward", "turn", "rotate", "project"]
        groups = tiles // GROUP
        xs_free = [early] * batches
        started = {}
        ff_jobs, ff_done = [], set()

        def feed_forward_stage():
            for job, name in list(ff_jobs):
                if next(job, "end") == "end":
                    ff_jobs.remove((job, name))
                    ff_done.add(name)
                    if name[1:] == (batches - 1, groups - 1) and name[0] + 2 < layers:
                        load_layer(name[0] + 2)

        def step(now):
            for stage in ORDER:
                if stage == "feed_forward":
                    feed_forward_stage()
                elif now - AGE[stage] in started:
                    job, (l, b, t) = started[now - AGE[stage]]
                    next(job, None)
                    if stage == "output" and t % GROUP == GROUP - 1:
                        ff_jobs.append((feed_forward(l, b, t // GROUP), (l, b, t // GROUP)))

        def finish_a():
            for _ in weighing:
                pass
            was_a.extend(a_state["end"])
            for b in range(batches):
                xf_zero[:] = [run("gpsimd", lambda e, b=b: e.memset(xfT[b][HEAD_DIM:P, 0:1], 0.0), was_a)]

        now = 0
        for l in range(layers):
            ready = load_qkv(l) if l else ready0
            for b in range(batches):
                for t in range(tiles):
                    if t % GROUP == 0:
                        while l and (l - 1, b, t // GROUP) not in ff_done:
                            step(now)
                            now += 1
                        xs_ready = shifted(xsT[b], b, t // GROUP, [], xs_free[b] + used["v"])
                    if l and (b, t) == (0, AGE["score"]):
                        ready["v"] = load("w_v", w_qkv[:, 2 * INNER:3 * INNER], ins["Wqkv"][l, :, 2 * INNER:3 * INNER], used["v"])
                    started[now] = attention_tile(l, b, t, ready, xs_ready), (l, b, t)
                    step(now)
                    now += 1
                    if l and (b, t) == (0, 0):
                        load_tables(l, ready)
                    if now == 1:
                        finish_a()
        while len(ff_done) < layers * batches * groups:
            step(now)
            now += 1

        stores = []
        YA = qk_sq.rearrange("p m (t d) -> p (m t) d", d=P)
        ya_loaded = load("ya_back", YA, scratch.rearrange("b (t p) d -> p (b t) d", p=P), was_a + st["sq"])
        for t0 in range(0, all_tiles, GROUP):
            g = slice(t0, t0 + GROUP)
            fin = run("vector", lambda e, g=g: e.tensor_tensor(YA[:, g, :], X[:, g, :], YA[:, g, :], ALU.add),
                      [ya_loaded] + [x_ready[t] for t in range(t0, t0 + GROUP)])
            b, first = divmod(t0, tiles)
            stores.append(load(f"out{t0 // GROUP}", out[b, P * first:P * (first + GROUP), :].rearrange("(t p) d -> p t d", p=P), YA[:, g, :], [fin]))
        prog.wait("sync", stores + was_a + [proj[k] for k in proj])
        with nc.Block() as block:
            prog.emit(block)


NAMES = {"L0_attn_Wq": "Wq", "L0_attn_Wk": "Wk", "L0_attn_Wv": "Wv", "L0_attn_W_O": "W_O", "L0_ffn_Wqkv": "Wqkv",
         "L0_ffn_q_scale": "q_scale", "L0_ffn_k_scale": "k_scale", "L0_ffn_Wo": "Wo", "L0_ffn_ln_g": "ln_g",
         "L0_ffn_ln_b": "ln_b", "L0_ffn_W1": "W1", "L0_ffn_b1": "b1", "L0_ffn_W2": "W2", "L0_ffn_b2": "b2",
         "L0_attn_x": "x"}


def kernel(**inputs):
    import concourse.bacc as bacc
    from concourse.bass_utils import run_bass_kernel_spmd

    nc = bacc.Bacc("TRN2", target_bir_lowering=False, num_devices=1)
    arrays = {short: np.ascontiguousarray(inputs[name]) for name, short in NAMES.items()}
    shape = arrays["x"].shape
    arrays["consts"] = mask_constants()
    arrays["tab_c"], arrays["tab_s"] = rotary_constants(shape[1])
    ins = {n: nc.dram_tensor(n, a.shape, mybir.dt.from_np(a.dtype), kind="ExternalInput").ap() for n, a in arrays.items()}
    out = nc.dram_tensor("out", shape, F32, kind="ExternalOutput").ap()
    scratch = nc.dram_tensor("scratch", shape, F32, kind="Internal").ap()
    parts_dram = nc.dram_tensor("parts_dram", [shape[0], 2, P, 3, shape[1]], BF16, kind="Internal").ap()
    build(nc, ins, out, scratch, parts_dram)
    result = run_bass_kernel_spmd(nc, [arrays], core_ids=[0])
    return result.results[0]["out"]
```
